# Optimizing a Trainium2 kernel written in Bass

```python
import numpy as np
import jax
import jax.numpy as jnp

def _softmax(x, axis=-1):
    return jax.nn.softmax(x, axis=axis)

def _gelu(x):
    return jax.nn.gelu(x, approximate=True)

def _silu(x):
    return jax.nn.silu(x)

def _sigmoid(x):
    return jax.nn.sigmoid(x)

def _layernorm(x, axis=-1, eps=1e-05):
    m = jnp.mean(x, axis=axis, keepdims=True)
    v = jnp.var(x, axis=axis, keepdims=True)
    return (x - m) / jnp.sqrt(v + eps)

def _scatter_add(tgt, idx, src, axis=0):
    return tgt.at[idx].add(src)

def _segment_sum(src, seg, n):
    return jax.ops.segment_sum(src, seg, n)
kernel_name = 'mk_rec_standalone_d1_rec_r8_2bf238'

def setup_inputs(seed: int=0):
    np.random.seed(seed)
    _w = jnp.asarray

    def _rec_inputs():
        import jax
        import jax.numpy as jnp
        _rk = jax.random.key(seed)
        r_behavior_emb = -0.000161372 + 0.999968 * jax.random.normal(jax.random.fold_in(_rk, 1), (512, 200, 128), jnp.float32)
        r_candidate_emb = 0.00222621 + 0.99962 * jax.random.normal(jax.random.fold_in(_rk, 2), (512, 128), jnp.float32)
        return (r_behavior_emb, r_candidate_emb)
    r_behavior_emb, r_candidate_emb = _rec_inputs()

    def _L0_rec_setup():
        import jax, jax.numpy as jnp
        import numpy as np
        B, S, E = (512, 200, 128)
        ATT_H, MLP_H = (128, 256)

        def _glorot(key, shape):
            fan_in, fan_out = (shape[0], shape[1])
            lim = np.sqrt(6.0 / (fan_in + fan_out)).astype(np.float32)
            return jax.random.uniform(key, shape, jnp.float32, -lim, lim)
        key = jax.random.key(seed)
        ks = jax.random.split(key, 10)
        return {'behavior_emb': jax.random.normal(ks[0], (B, S, E), jnp.float32), 'candidate_emb': jax.random.normal(ks[1], (B, E), jnp.float32), 'fc1_w': _glorot(ks[2], (2 * E, ATT_H)), 'fc1_b': jnp.zeros((ATT_H,), jnp.float32), 'fc2_w': _glorot(ks[3], (ATT_H, 1)), 'fc2_b': jnp.zeros((1,), jnp.float32), 'mlp1_w': _glorot(ks[4], (2 * E, MLP_H)), 'mlp1_b': jnp.zeros((MLP_H,), jnp.float32), 'mlp2_w': _glorot(ks[5], (MLP_H, 1)), 'mlp2_b': jnp.zeros((1,), jnp.float32)}
    _L0_rec_all = _L0_rec_setup()
    _L0_rec_in = {k: v for k, v in _L0_rec_all.items() if k in ('fc1_w', 'fc1_b', 'fc2_w', 'fc2_b', 'mlp1_w', 'mlp1_b', 'mlp2_w', 'mlp2_b')}
    del _L0_rec_all
    return {'r_behavior_emb': r_behavior_emb, 'r_candidate_emb': r_candidate_emb, 'L0_rec_fc1_w': _L0_rec_in['fc1_w'], 'L0_rec_fc1_b': _L0_rec_in['fc1_b'], 'L0_rec_fc2_w': _L0_rec_in['fc2_w'], 'L0_rec_fc2_b': _L0_rec_in['fc2_b'], 'L0_rec_mlp1_w': _L0_rec_in['mlp1_w'], 'L0_rec_mlp1_b': _L0_rec_in['mlp1_b'], 'L0_rec_mlp2_w': _L0_rec_in['mlp2_w'], 'L0_rec_mlp2_b': _L0_rec_in['mlp2_b']}

def reference(r_behavior_emb, r_candidate_emb, L0_rec_fc1_w, L0_rec_fc1_b, L0_rec_fc2_w, L0_rec_fc2_b, L0_rec_mlp1_w, L0_rec_mlp1_b, L0_rec_mlp2_w, L0_rec_mlp2_b):
    import jax
    import jax.numpy as jnp

    def _L0_rec_ref(behavior_emb, candidate_emb, fc1_w, fc1_b, fc2_w, fc2_b, mlp1_w, mlp1_b, mlp2_w, mlp2_b):
        import jax, jax.numpy as jnp
        import numpy as np
        B, S, E = (512, 200, 128)
        ATT_H, MLP_H = (128, 256)

        def _glorot(key, shape):
            fan_in, fan_out = (shape[0], shape[1])
            lim = np.sqrt(6.0 / (fan_in + fan_out)).astype(np.float32)
            return jax.random.uniform(key, shape, jnp.float32, -lim, lim)
        W_b, W_c = (fc1_w[:E], fc1_w[E:])
        h = jax.nn.relu(jnp.einsum('bse,eh->bsh', behavior_emb, W_b) + (candidate_emb @ W_c)[:, None, :] + fc1_b)
        scores = jnp.einsum('bsh,h->bs', h, fc2_w[:, 0]) + fc2_b[0]
        attn = jax.nn.softmax(scores, axis=-1)
        user_interest = jnp.einsum('bse,bs->be', behavior_emb, attn)
        x = jnp.concatenate([user_interest, candidate_emb], axis=1)
        z = jax.nn.relu(x @ mlp1_w + mlp1_b)
        logit = (z @ mlp2_w + mlp2_b)[:, 0]
        return logit
    y = _L0_rec_ref(r_behavior_emb, r_candidate_emb, L0_rec_fc1_w, L0_rec_fc1_b, L0_rec_fc2_w, L0_rec_fc2_b, L0_rec_mlp1_w, L0_rec_mlp1_b, L0_rec_mlp2_w, L0_rec_mlp2_b)
    return y

_drawn_inputs = setup_inputs


def setup_inputs(seed=0):
    import zlib

    import numpy as np

    out = dict(_drawn_inputs(seed))
    spreads = {'L0_rec_fc1_b': (0.0, 0.8), 'L0_rec_mlp1_b': (0.0, 0.1)}
    factors = {}
    for name, (base, spread) in spreads.items():
        noise = np.random.default_rng([zlib.crc32(name.encode()), seed]).standard_normal(out[name].shape)
        drawn = base * np.exp(spread * noise) if base else spread * noise
        out[name] = jnp.asarray(drawn.astype(out[name].dtype))
    for name, factor in factors.items():
        out[name] = (out[name] * factor).astype(out[name].dtype)
    return out
```

```python
from contextlib import ExitStack

import concourse.bass as bass
from concourse import mybir

F32 = mybir.dt.float32
F32R = mybir.dt.float32r
ALU = mybir.AluOpType
ACT = mybir.ActivationFunctionType
AX = mybir.AxisListType

P = 128
PARTS = 8
GROUPS = [4, 4, 4, 4, 3, 3, 3]
NG = len(GROUPS)
STARTS = [sum(GROUPS[:k]) for k in range(NG)]
X_BUFS = 4
SPLIT_BUFS = 4
Z_BANKS = 4
T_BANKS = 2
Q = 32
AHEAD = 2


def attention_pooling_kernel(nc, behavior, candidate, fc1_w, fc1_b, fc2_w, fc2_b,
                             mlp1_w, mlp1_b, mlp2_w, mlp2_b, layout, out):
    B, S, E = behavior.shape
    H = fc1_w.shape[1]
    H2 = mlp1_w.shape[1]
    assert E == P and H == P and H2 == 2 * P and S % PARTS == 0
    TILES = S // PARTS
    ROWS = P // PARTS
    CHUNKS = B // ROWS
    NB = B // P
    assert sum(GROUPS) == TILES and CHUNKS % X_BUFS == 0
    RUN = (TILES + 1) // 2
    RUN_START = [0, TILES - RUN]
    LOTS = [(0, 12), (12, TILES)]

    behavior_v = behavior.rearrange("(c r) (a t) e -> c (r a) (t e)", r=ROWS, a=PARTS)
    out_v = out.rearrange("(a b) -> a b", a=1)

    with ExitStack() as ctx:
        def sb(name, shape, dt=F32):
            return ctx.enter_context(nc.sbuf_tensor(name, shape, dt))

        def sem(name):
            return ctx.enter_context(nc.semaphore(name))

        x = [sb(f"x{i}", [P, TILES * E]) for i in range(X_BUFS)]
        xh = [sb(f"xh{i}", [P, 4 * P], F32R) for i in range(SPLIT_BUFS)]
        xl = [sb(f"xl{i}", [P, 4 * P], F32R) for i in range(SPLIT_BUFS)]
        hidden = [sb(f"hidden{i}", [P, TILES, P]) for i in range(2)]
        scores = [sb(f"scores{i}", [P, RUN * Q]) for i in range(2)]
        part_max = sb("part_max", [P, Q])
        part_max_t = sb("part_max_t", [P, Q])
        row_max_t = sb("row_max_t", [P, Q // PARTS])
        row_max_wide = sb("row_max_wide", [P, Q])
        row_max = sb("row_max", [P, Q])
        exp_bias = [sb(f"exp_bias{i}", [P, 1]) for i in range(2)]
        weights = [sb(f"weights{i}", [P, TILES]) for i in range(2)]
        weights_by_row = [sb(f"weights_by_row{i}", [P, TILES, ROWS]) for i in range(2)]
        weight_sums = sb("weight_sums", [P, CHUNKS, 2])
        pooled4 = sb("pooled4", [P, P])
        pooled_t = sb("pooled_t", [P, B])
        cand = sb("cand", [P, NB, E])
        cand_t = sb("cand_t", [P, B])
        w_b = sb("w_b", [P, H])
        w_c = sb("w_c", [P, H])
        w_hi = sb("w_hi", [P, H], F32R)
        w_lo = sb("w_lo", [P, H], F32R)
        b1 = sb("b1", [P, 1])
        f2 = sb("f2", [P, 1])
        f2_col = sb("f2_col", [P, 2 * Q])
        b2 = sb("b2", [P, 1])
        w_mlp = sb("w_mlp", [P, 2, H2])
        b_mlp = sb("b_mlp", [P, 2])
        w_out = sb("w_out", [P, 2])
        b_out = sb("b_out", [1, 1])
        lay = sb("lay", [P, P + 2 * ROWS])
        ident = lay[:, 0:P]
        row_mask = lay[:, P:P + ROWS]
        fold = lay[:, P + ROWS:P + 2 * ROWS]
        ones = sb("ones", [P, P])
        neg_bias = sb("neg_bias", [P, B])
        bias_f2 = sb("bias_f2", [P, B])
        shift_sel = sb("shift_sel", [P, CHUNKS, ROWS])
        shift = sb("shift", [P, CHUNKS])
        z_cand = sb("z_cand", [P, 2, B])
        sums = sb("sums", [P, CHUNKS])
        sums_sel = sb("sums_sel", [P, CHUNKS, ROWS])
        inv_sum = sb("inv_sum", [P, B])
        pooled_n = sb("pooled_n", [P, B])
        z_all = sb("z_all", [P, 2, B])
        logit = sb("logit", [1, B])

        xt_ps = [ctx.enter_context(nc.psum_tensor(f"xt_ps{i}", [P, 512], F32)) for i in range(T_BANKS)]
        z_ps = [ctx.enter_context(nc.psum_tensor(f"z_ps{i}", [P, 512], F32)) for i in range(Z_BANKS)]
        s_ps = ctx.enter_context(nc.psum_tensor("s_ps", [P, 512], F32))
        u_ps = ctx.enter_context(nc.psum_tensor("u_ps", [P, 512], F32))

        x_first = sem("x_first")
        x_loaded = [sem(f"x_loaded{i}") for i in range(X_BUFS)]
        lay_loaded = sem("lay_loaded")
        fc_loaded = sem("fc_loaded")
        cand_loaded = sem("cand_loaded")
        mlp_loaded = sem("mlp_loaded")
        consts_made = sem("consts_made")
        w_hi_made = sem("w_hi_made")
        w_lo_made = sem("w_lo_made")
        cand_t_done = sem("cand_t_done")
        cand_t_copied = sem("cand_t_copied")
        bias_done = sem("bias_done")
        setup_step = sem("setup_step")
        bias_f2_made = sem("bias_f2_made")
        shift_done = sem("shift_done")
        shift_made = sem("shift_made")
        z_cand_done = sem("z_cand_done")
        z_cand_copied = sem("z_cand_copied")
        transposed = sem("transposed")
        xh_made = sem("xh_made")
        xl_made = sem("xl_made")
        z_done = sem("z_done")
        hidden_made = sem("hidden_made")
        scores_done = sem("scores_done")
        softmax_step = sem("softmax_step")
        weights_made = sem("weights_made")
        weights_masked = sem("weights_masked")
        pooled_done = sem("pooled_done")
        pooled4_copied = sem("pooled4_copied")
        pooled_t_done = sem("pooled_t_done")
        pooled_t_copied = sem("pooled_t_copied")
        tail_step = sem("tail_step")
        sums_done = sem("sums_done")
        z_all_done = sem("z_all_done")
        z_all_relu = sem("z_all_relu")
        logit_done = sem("logit_done")
        logit_made = sem("logit_made")
        stored = sem("stored")

        SOFTMAX_STEPS = 7

        def periods(eng, body):
            for c in range(2):
                body(c, c % X_BUFS, c)
            with eng.Fori(0, (CHUNKS - 4) // X_BUFS) as turn:
                for j in range(X_BUFS):
                    body(turn * X_BUFS + (2 + j), (2 + j) % X_BUFS, 2)
            for c in range(CHUNKS - 2, CHUNKS):
                body(c, c % X_BUFS, c)

        def slot(q, k, n):
            return (q * NG + k) % n

        def hidden_view(buf, k):
            return hidden[buf][:, STARTS[k]:STARTS[k] + GROUPS[k], :].rearrange("p t (b s) -> p t b s", s=PARTS)

        def score_runs(buf):
            return scores[buf][:, :].rearrange("p (t r) -> p r t", r=Q)[:, 0:2, :]

        block = ctx.enter_context(nc.Block())

        @block.sync
        def _(sp):
            cut = GROUPS[0] * E
            sp.dma_start(x[0][:, 0:cut], behavior_v[0, :, 0:cut]).then_inc(x_first, 16)
            sp.dma_start(x[0][:, cut:], behavior_v[0, :, cut:]).then_inc(x_loaded[0], 16)
            for c in range(1, X_BUFS):
                sp.dma_start(x[c][:, :], behavior_v[c]).then_inc(x_loaded[c], 16)
            with sp.Fori(0, CHUNKS // X_BUFS - 1) as turn:
                for j in range(X_BUFS):
                    sp.wait_ge(pooled_done, turn * X_BUFS + (j + 1))
                    sp.dma_start(x[j][:, :], behavior_v[turn * X_BUFS + (X_BUFS + j)]).then_inc(x_loaded[j], 16)
            sp.wait_ge(logit_made, 1)
            sp.dma_start(out_v, logit[:, :]).then_inc(stored, 16)
            sp.wait_ge(stored, 16)

        @block.gpsimd
        def _(pool):
            nc.gpsimd.memset(ones[:, :], 1.0).then_inc(consts_made, 1)
            pool.wait_ge(lay_loaded, 16)

            def mask_weights(c, buf, first):
                pool.wait_ge(weights_made, c * 2 + 2)
                if not first:
                    pool.wait_ge(pooled_done, c - 1)
                nc.gpsimd.tensor_tensor(
                    weights_by_row[buf][:, :, :],
                    weights[buf][:, :].unsqueeze(2).to_broadcast([P, TILES, ROWS]),
                    row_mask.unsqueeze(1).to_broadcast([P, TILES, ROWS]),
                    ALU.mult).then_inc(weights_masked, 1)

            for c in range(2):
                mask_weights(c, c, True)
            with pool.Fori(0, CHUNKS // 2 - 1) as turn:
                for j in range(2):
                    mask_weights(turn * 2 + (2 + j), j, False)

        @block.scalar
        def _(act):
            act.dma_start(lay[:, :], layout).then_inc(lay_loaded, 16)
            act.dma_start(cand[:, :, :], candidate.rearrange("(n p) e -> p n e", p=P)).then_inc(cand_loaded, 16)
            act.dma_start(w_b[:, :], fc1_w[0:E, :]).then_inc(fc_loaded, 16)
            act.dma_start(w_c[:, :], fc1_w[E:2 * E, :]).then_inc(fc_loaded, 16)
            with nc.allow_non_contiguous_dma(reason="vectors onto partitions, once"):
                act.dma_start(b1[:, :], fc1_b.rearrange("(h a) -> h a", a=1)).then_inc(fc_loaded, 16)
                act.dma_start(f2[:, :], fc2_w).then_inc(fc_loaded, 16)
                act.dma_start(b2[:, :], fc2_b.rearrange("(h a) -> h a", a=1).to_broadcast([P, 1])).then_inc(fc_loaded, 16)
                act.dma_start(w_mlp[:, :, :], mlp1_w.rearrange("(n p) h -> p n h", p=P)).then_inc(mlp_loaded, 16)
                act.dma_start(b_mlp[:, :], mlp1_b.rearrange("(n p) -> p n", p=P)).then_inc(mlp_loaded, 16)
                act.dma_start(w_out[:, :], mlp2_w.rearrange("(n p) a -> p (n a)", p=P)).then_inc(mlp_loaded, 16)
                act.dma_start(b_out[:, :], mlp2_b.rearrange("(h a) -> h a", a=1)).then_inc(mlp_loaded, 16)
            act.wait_ge(fc_loaded, 16 * 5)
            nc.scalar.copy(w_hi[:, :], w_b[:, :]).then_inc(w_hi_made, 1)
            act.wait_ge(cand_t_done, 1)
            nc.scalar.copy(cand_t[:, :], s_ps[:, :]).then_inc(cand_t_copied, 1)
            act.wait_ge(mlp_loaded, 16 * 4)
            for m in range(2):
                act.wait_ge(z_cand_done, m + 1)
                nc.scalar.activation(z_cand[:, m, :], z_ps[m][:, :], ACT.Identity,
                                     bias=b_mlp[:, m:m + 1]).then_inc(z_cand_copied, 1)

            def high_half(c, q, k, early):
                w = GROUPS[k] * P
                act.wait_ge(transposed, c * NG + (k + 1))
                if not early:
                    act.wait_ge(z_done, c * NG + (k + 1 - SPLIT_BUFS))
                nc.scalar.copy(xh[slot(q, k, SPLIT_BUFS)][:, 0:w],
                               xt_ps[slot(q, k, T_BANKS)][:, 0:w]).then_inc(xh_made, 1)

            def exponents(c, buf, early):
                act.wait_ge(softmax_step, c * SOFTMAX_STEPS + SOFTMAX_STEPS)
                if not early:
                    act.wait_ge(weights_masked, c - 1)
                runs = score_runs(buf)
                nc.scalar.activation(weights[buf][:, 0:RUN], runs[:, 0, :], ACT.Exp, bias=exp_bias[buf][:, :],
                                     accum_out=weight_sums[:, c, 0:1]).then_inc(weights_made, 1)
                skip = 2 * RUN - TILES
                nc.scalar.activation(weights[buf][:, RUN:TILES], runs[:, 1, skip:RUN], ACT.Exp,
                                     bias=exp_bias[buf][:, :],
                                     accum_out=weight_sums[:, c, 1:2]).then_inc(weights_made, 1)

            def copy_pooled4(c, first):
                act.wait_ge(pooled_done, c + 1)
                if not first:
                    act.wait_ge(pooled_t_done, c)
                nc.scalar.copy(pooled4[:, :], u_ps[:, 0:P]).then_inc(pooled4_copied, 1)

            def copy_pooled_t(c):
                act.wait_ge(pooled_t_done, c + 1)
                nc.scalar.copy(pooled_t[:, bass.ds(c * ROWS, ROWS)], u_ps[:, P:P + ROWS]).then_inc(pooled_t_copied, 1)

            for k in range(AHEAD):
                high_half(0, 0, k, True)

            def period(c, q, phase):
                for k in range(NG):
                    if k + AHEAD < NG:
                        high_half(c, q, k + AHEAD, phase == 0 and k + AHEAD < SPLIT_BUFS)
                    elif phase != CHUNKS - 1:
                        high_half(c + 1, (q + 1) % X_BUFS, k + AHEAD - NG, False)
                    if k == 4 and phase >= 2:
                        copy_pooled4(c - 2, phase == 2 and isinstance(c, int) and c == 2)
                    if k == 5 and phase >= 2:
                        copy_pooled_t(c - 2)
                    if k == 6 and phase >= 1:
                        exponents(c - 1, (q + 1) % 2, phase <= 2 and isinstance(c, int))

            periods(act, period)
            copy_pooled4(CHUNKS - 2, False)
            copy_pooled_t(CHUNKS - 2)
            exponents(CHUNKS - 1, (CHUNKS - 1) % 2, False)
            copy_pooled4(CHUNKS - 1, False)
            copy_pooled_t(CHUNKS - 1)
            for m in range(2):
                act.wait_ge(tail_step, 5 + m)
                nc.scalar.activation(z_all[:, m, :], z_all[:, m, :], ACT.Relu).then_inc(z_all_relu, 1)

        @block.vector
        def _(dve):
            nc.vector.memset(f2_col[:, :], 0.0).then_inc(setup_step, 1)
            nc.vector.memset(part_max[:, :], 0.0).then_inc(consts_made, 1)
            nc.vector.memset(u_ps[:, 0:P], 0.0).then_inc(consts_made, 1)
            dve.wait_ge(fc_loaded, 16 * 5)
            dve.wait_ge(setup_step, 1)
            nc.vector.tensor_copy(f2_col[:, Q:Q + 1], f2[:, :]).then_inc(consts_made, 1)
            dve.wait_ge(w_hi_made, 1)
            nc.vector.tensor_tensor(w_lo[:, :], w_b[:, :], w_hi[:, :].bitcast(F32), ALU.subtract).then_inc(w_lo_made, 1)
            dve.wait_ge(bias_done, 1)
            nc.vector.tensor_scalar(neg_bias[:, :], z_ps[2][:, :], b1[:, :], -1.0, ALU.add, ALU.mult).then_inc(setup_step, 1)
            dve.wait_ge(setup_step, 2)
            nc.vector.tensor_scalar(bias_f2[:, :], neg_bias[:, :], f2[:, :], -1.0, ALU.mult, ALU.mult).then_inc(bias_f2_made, 1)
            dve.wait_ge(shift_done, 1)
            dve.wait_ge(lay_loaded, 16)
            nc.vector.tensor_tensor(shift_sel[:, :, :], z_ps[3][:, :].rearrange("p (c r) -> p c r", r=ROWS),
                                    row_mask.unsqueeze(1).to_broadcast([P, CHUNKS, ROWS]), ALU.mult).then_inc(setup_step, 1)
            dve.wait_ge(setup_step, 3)
            nc.vector.reduce_sum(shift[:, :], shift_sel[:, :, :], axis=AX.X).then_inc(setup_step, 1)
            dve.wait_ge(setup_step, 4)
            nc.vector.tensor_scalar(shift[:, :], shift[:, :], b2[:, :], None, ALU.add).then_inc(shift_made, 1)

            def low_half(c, q, k):
                w = GROUPS[k] * P
                h = xh[slot(q, k, SPLIT_BUFS)][:, 0:w]
                dve.wait_ge(xh_made, c * NG + (k + 1))
                nc.vector.tensor_tensor(xl[slot(q, k, SPLIT_BUFS)][:, 0:w], xt_ps[slot(q, k, T_BANKS)][:, 0:w],
                                        h.bitcast(F32), ALU.subtract).then_inc(xl_made, 1)

            def biased_max(c, q, k, early):
                t = GROUPS[k]
                dve.wait_ge(z_done, c * NG + (k + 1))
                if k == 0 and not early:
                    dve.wait_ge(scores_done, c - 1)
                z = z_ps[slot(q, k, Z_BANKS)][:, 0:t * P].rearrange("p (t b s) -> p t b s", b=ROWS, s=PARTS)
                nb = neg_bias[:, bass.ds(c * ROWS, ROWS)].unsqueeze(1).unsqueeze(3)
                nc.vector.tensor_tensor(hidden_view(q % 2, k), z, nb.to_broadcast([P, t, ROWS, PARTS]),
                                        ALU.max).then_inc(hidden_made, 1)

            def softmax(c, buf, step, early):
                done = c * SOFTMAX_STEPS + step
                if step == 0:
                    dve.wait_ge(scores_done, c + 1)
                    if not early:
                        dve.wait_ge(weights_made, c * 2 - 2)
                    op = nc.vector.transpose(scores[buf][:, :], s_ps[:, 0:RUN * Q])
                else:
                    dve.wait_ge(softmax_step, done)
                if step == 1:
                    op = nc.vector.tensor_reduce(part_max[:, 0:1], score_runs(buf), axis=AX.XY, op=ALU.max)
                if step == 2:
                    op = nc.vector.transpose(part_max_t[:, :], part_max[:, :])
                if step == 3:
                    op = nc.vector.tensor_reduce(row_max_t[:, :], part_max_t[:, :].rearrange("p (b s) -> p b s", s=PARTS),
                                                 axis=AX.X, op=ALU.max)
                if step == 4:
                    op = nc.vector.tensor_copy(row_max_wide[:, :].rearrange("p (b s) -> p b s", s=PARTS),
                                               row_max_t[:, :].unsqueeze(2).to_broadcast([P, Q // PARTS, PARTS]))
                if step == 5:
                    op = nc.vector.transpose(row_max[:, :], row_max_wide[:, :])
                if step == 6:
                    own = shift[:, bass.ds(c, 1)]
                    op = nc.vector.scalar_tensor_tensor(exp_bias[buf][:, :], row_max[:, 0:1], own, own,
                                                        ALU.add, ALU.subtract, reverse1=True)
                op.then_inc(softmax_step, 1)

            dve.wait_ge(shift_made, 1)
            low_half(0, 0, 0)

            def period(c, q, phase):
                for k in range(NG):
                    if k + 1 < NG:
                        low_half(c, q, k + 1)
                    elif phase != CHUNKS - 1:
                        low_half(c + 1, (q + 1) % X_BUFS, 0)
                    if phase >= 1 and 2 <= k <= 5:
                        softmax(c - 1, (q + 1) % 2, 2 * (k - 2), isinstance(c, int) and phase <= 2)
                    biased_max(c, q, k, phase < 2)
                    if phase >= 1 and 2 <= k <= 4:
                        softmax(c - 1, (q + 1) % 2, 2 * (k - 2) + 1, isinstance(c, int) and phase <= 2)

            periods(dve, period)
            last = CHUNKS - 1
            for step in range(SOFTMAX_STEPS):
                softmax(last, last % 2, step, False)
            dve.wait_ge(weights_made, 2 * CHUNKS)
            nc.vector.tensor_tensor(sums[:, :], weight_sums[:, :, 0], weight_sums[:, :, 1], ALU.add).then_inc(tail_step, 1)
            dve.wait_ge(tail_step, 1)
            nc.vector.tensor_tensor(sums_sel[:, :, :], sums[:, :].unsqueeze(2).to_broadcast([P, CHUNKS, ROWS]),
                                    row_mask.unsqueeze(1).to_broadcast([P, CHUNKS, ROWS]), ALU.mult).then_inc(tail_step, 1)
            dve.wait_ge(sums_done, 1)
            nc.vector.reciprocal(inv_sum[:, :], z_ps[2][:, :]).then_inc(tail_step, 1)
            dve.wait_ge(tail_step, 3)
            dve.wait_ge(pooled_t_copied, CHUNKS)
            nc.vector.tensor_tensor(pooled_n[:, :], pooled_t[:, :], inv_sum[:, :], ALU.mult).then_inc(tail_step, 1)
            for m in range(2):
                dve.wait_ge(z_all_done, m + 1)
                nc.vector.tensor_tensor(z_all[:, m, :], z_ps[m][:, :], z_cand[:, m, :], ALU.add).then_inc(tail_step, 1)
            dve.wait_ge(logit_done, 1)
            nc.vector.tensor_scalar(logit[:, :], s_ps[0:1, :], b_out[:, :], None, ALU.add).then_inc(logit_made, 1)

        @block.tensor
        def _(pe):
            pe.wait_ge(lay_loaded, 16)
            pe.wait_ge(cand_loaded, 16)
            for n in range(NB):
                op = nc.tensor.transpose(s_ps[:, n * P:(n + 1) * P], cand[:, n, :], ident)
            op.then_inc(cand_t_done, 1)
            pe.wait_ge(fc_loaded, 16 * 5)
            pe.wait_ge(cand_t_copied, 1)
            nc.tensor.matmul(z_ps[2][:, :], w_c[:, :], cand_t[:, :], start=True, stop=True).then_inc(bias_done, 1)
            pe.wait_ge(mlp_loaded, 16 * 4)
            for m in range(2):
                nc.tensor.matmul(z_ps[m][:, :], w_mlp[:, 1, m * P:(m + 1) * P], cand_t[:, :],
                                 start=True, stop=True).then_inc(z_cand_done, 1)
            pe.wait_ge(consts_made, 4)
            pe.wait_ge(bias_f2_made, 1)
            nc.tensor.matmul(z_ps[3][:, :], ones[:, :], bias_f2[:, :], start=True, stop=True).then_inc(shift_done, 1)
            pe.wait_ge(z_cand_copied, 2)
            pe.wait_ge(w_lo_made, 1)

            def transpose(c, q, k, loaded, early):
                if loaded is not None:
                    pe.wait_ge(loaded[0], loaded[1])
                if not early:
                    pe.wait_ge(xl_made, c * NG + (k + 1 - T_BANKS))
                for j in range(GROUPS[k]):
                    t = STARTS[k] + j
                    op = nc.tensor.transpose(xt_ps[slot(q, k, T_BANKS)][:, j * P:(j + 1) * P],
                                             x[q][:, t * E:(t + 1) * E], ident)
                op.then_inc(transposed, 1)

            def products(c, q, k, early):
                w = GROUPS[k] * P
                s = slot(q, k, SPLIT_BUFS)
                z = z_ps[slot(q, k, Z_BANKS)][:, 0:w]
                pe.wait_ge(xl_made, c * NG + (k + 1))
                if not early:
                    pe.wait_ge(hidden_made, c * NG + (k + 1 - Z_BANKS))
                nc.tensor.matmul(z, w_hi[:, :], xh[s][:, 0:w], start=True, stop=False)
                nc.tensor.matmul(z, w_lo[:, :], xh[s][:, 0:w], start=False, stop=False)
                nc.tensor.matmul(z, w_hi[:, :], xl[s][:, 0:w], start=False, stop=True).then_inc(z_done, 1)

            def score(c, buf, first):
                pe.wait_ge(hidden_made, c * NG + NG)
                if not first:
                    pe.wait_ge(softmax_step, c * SOFTMAX_STEPS - (SOFTMAX_STEPS - 1))
                for r in range(2):
                    for g in range(P // Q):
                        op = nc.tensor.matmul(
                            s_ps[g * Q:(g + 1) * Q, 0:RUN * Q].rearrange("p (t s) -> p t s", s=Q),
                            f2_col[:, Q - r:2 * Q - r],
                            hidden[buf][:, RUN_START[r]:RUN_START[r] + RUN, g * Q:(g + 1) * Q],
                            start=(r == 0), stop=(r == 1), tile_position=(0, g * Q))
                op.then_inc(scores_done, 1)

            def weighted_sum(c, q, lot, first):
                if lot == 0:
                    pe.wait_ge(weights_masked, c + 1)
                    if not first:
                        pe.wait_ge(pooled_t_copied, c)
                for t in range(*LOTS[lot]):
                    g = t % (P // Q)
                    op = nc.tensor.matmul(u_ps[g * Q:g * Q + ROWS, 0:P], weights_by_row[q % 2][:, t, :],
                                          x[q][:, t * E:(t + 1) * E], start=(t < P // Q),
                                          stop=(t >= TILES - P // Q), tile_position=(0, g * Q))
                if lot == len(LOTS) - 1:
                    op.then_inc(pooled_done, 1)

            def transpose_sums(c):
                pe.wait_ge(pooled4_copied, c + 1)
                nc.tensor.matmul(u_ps[:, P:P + ROWS], pooled4[:, :], fold, start=True, stop=True).then_inc(pooled_t_done, 1)

            transpose(0, 0, 0, (x_first, 16), True)
            transpose(0, 0, 1, (x_loaded[0], 16), True)

            def period(c, q, phase):
                for k in range(NG):
                    products(c, q, k, phase == 0 and k < Z_BANKS)
                    if k + AHEAD < NG:
                        transpose(c, q, k + AHEAD, None, False)
                    elif phase != CHUNKS - 1:
                        nq = (q + 1) % X_BUFS
                        if isinstance(c, int):
                            loads = 16 * ((c + 1) // X_BUFS + 1)
                        else:
                            loads = turn_loads(c, q)
                        transpose(c + 1, nq, k + AHEAD - NG, (x_loaded[nq], loads) if k == NG - AHEAD else None, False)
                    if k == 1 and phase >= 1:
                        score(c - 1, (q + 1) % 2, phase == 1)
                    if k == 1 and phase >= 2:
                        weighted_sum(c - 2, (q + 2) % X_BUFS, 0, isinstance(c, int) and c == 2)
                    if k == 4 and phase >= 2:
                        weighted_sum(c - 2, (q + 2) % X_BUFS, 1, False)
                    if k == 5 and phase >= 2:
                        transpose_sums(c - 2)

            def turn_loads(c, q):
                return (c + (1 + X_BUFS - (q + 1) % X_BUFS)) * (16 // X_BUFS)

            periods(pe, period)
            last = CHUNKS - 1
            score(last, last % 2, False)
            for lot in range(len(LOTS)):
                weighted_sum(last - 1, (last - 1) % X_BUFS, lot, False)
            transpose_sums(last - 1)
            pe.wait_ge(tail_step, 2)
            nc.tensor.matmul(z_ps[2][:, :], ones[:, :], sums_sel[:, :, :].rearrange("p c r -> p (c r)"),
                             start=True, stop=True).then_inc(sums_done, 1)
            for lot in range(len(LOTS)):
                weighted_sum(last, last % X_BUFS, lot, False)
            transpose_sums(last)
            pe.wait_ge(tail_step, 4)
            for m in range(2):
                nc.tensor.matmul(z_ps[m][:, :], w_mlp[:, 0, m * P:(m + 1) * P], pooled_n[:, :],
                                 start=True, stop=True).then_inc(z_all_done, 1)
            for m in range(2):
                pe.wait_ge(z_all_relu, m + 1)
                op = nc.tensor.matmul(s_ps[0:1, :], w_out[:, m:m + 1], z_all[:, m, :], start=(m == 0), stop=(m == 1))
            op.then_inc(logit_done, 1)


_INS = ["r_behavior_emb", "r_candidate_emb", "L0_rec_fc1_w", "L0_rec_fc1_b", "L0_rec_fc2_w", "L0_rec_fc2_b",
        "L0_rec_mlp1_w", "L0_rec_mlp1_b", "L0_rec_mlp2_w", "L0_rec_mlp2_b"]


def layout_constants():
    import numpy as np

    p = np.arange(P)[:, None]
    rows = np.arange(P // PARTS)[None, :]
    return np.concatenate([p == np.arange(P)[None, :], p // PARTS == rows, p % Q == rows], axis=1).astype(np.float32)


def kernel(**inputs):
    import numpy as np
    import concourse.bacc as bacc
    from concourse.bass_utils import run_bass_kernel_spmd

    nc = bacc.Bacc("TRN2", target_bir_lowering=False, num_devices=1)
    arrays, args = {}, []
    for name in _INS:
        arrays[f"in_{name}"] = np.ascontiguousarray(inputs[name])
    arrays["in_layout"] = layout_constants()
    for name, a in arrays.items():
        args.append(nc.dram_tensor(name, a.shape, mybir.dt.from_np(a.dtype), kind="ExternalInput").ap())
    rows = inputs["r_behavior_emb"].shape[0]
    args.append(nc.dram_tensor("out_logit", (rows,), F32, kind="ExternalOutput").ap())
    attention_pooling_kernel(nc, *args)
    r = run_bass_kernel_spmd(nc, [arrays], core_ids=[0])
    return r.results[0]["out_logit"]
```

```python
from contextlib import ExitStack

import concourse.bass as bass
from concourse import mybir

F32 = mybir.dt.float32
F32R = mybir.dt.float32r
ALU = mybir.AluOpType
ACT = mybir.ActivationFunctionType
AX = mybir.AxisListType

P = 128
PARTS = 8
GROUPS = [4, 4, 4, 4, 3, 3, 3]
NG = len(GROUPS)
STARTS = [sum(GROUPS[:k]) for k in range(NG)]
X_BUFS = 4
SCALAR_TILES = [5, 2, 2, 1, 1, 1, 0]
BY_SCALAR = sum(SCALAR_TILES)
BY_POOL = 21 - BY_SCALAR
SUMMED = 4
SPLIT_BUFS = 4
Z_BANKS = 3
T_BANKS = 3
Q = 32
AHEAD = 3
LOW_AHEAD = 2
TAIL = 4


def rotation(n):
    count = X_BUFS * NG
    slots = [g % n for g in range(count)]
    if count % n == 1:
        slots[-1] = 1
    else:
        assert count % n == 0
    twice = slots + slots
    back = [next(d for d in range(1, count) if twice[count + g - d] == slots[g]) for g in range(count)]
    return slots, back


ROTATION = {n: rotation(n) for n in (SPLIT_BUFS, Z_BANKS, T_BANKS)}


def slot(q, k, n):
    return ROTATION[n][0][q * NG + k]


def back(q, k, n):
    return ROTATION[n][1][q * NG + k]


FIRST_COLS = {"ident": P, "row_mask": P // PARTS, "fold": P // PARTS, "row_first": P // PARTS, "same_row": P,
              "w_b": P, "w_c": P, "b1": 1, "f2": 1, "b2": 1}
LATER_COLS = {"w_mlp": 4 * P, "b_mlp": 2, "w_out": 2, "b_out": 1}


def attention_pooling_kernel(nc, behavior, candidate, first, later, out):
    B, S, E = behavior.shape
    H = P
    assert E == P and S % PARTS == 0
    TILES = S // PARTS
    ROWS = P // PARTS
    CHUNKS = B // ROWS
    NB = B // P
    assert sum(GROUPS) == TILES and CHUNKS % X_BUFS == 0 and X_BUFS == 4
    RUN = (TILES + 1) // 2
    RUN_START = [0, TILES - RUN]
    FIRST_RUN_GROUPS = next(k for k in range(NG) if STARTS[k] >= RUN)
    PART_CHUNKS = [(0, CHUNKS - TAIL), (CHUNKS - TAIL, CHUNKS)]
    DIRECT = BY_SCALAR + BY_POOL
    assert TILES - DIRECT == SUMMED == P // Q and STARTS[5] < DIRECT < STARTS[6]

    behavior_v = behavior.rearrange("(c r) (a t) e -> c (r a) (t e)", r=ROWS, a=PARTS)
    out_v = out.rearrange("(a b) -> a b", a=1)

    with ExitStack() as ctx:
        def sb(name, shape, dt=F32):
            return ctx.enter_context(nc.sbuf_tensor(name, shape, dt))

        def sem(name):
            return ctx.enter_context(nc.semaphore(name))

        x = [sb(f"x{i}", [P, TILES * E]) for i in range(X_BUFS)]
        xh = [sb(f"xh{i}", [P, 4 * P], F32R) for i in range(SPLIT_BUFS)]
        xl = [sb(f"xl{i}", [P, 4 * P], F32R) for i in range(SPLIT_BUFS)]
        hidden = [sb(f"hidden{i}", [P, TILES, P]) for i in range(2)]
        scores = [sb(f"scores{i}", [P, RUN * Q]) for i in range(2)]
        part_max = sb("part_max", [P, Q])
        part_max_t = sb("part_max_t", [P, Q])
        row_max_t = sb("row_max_t", [P, Q // PARTS])
        row_max_wide = sb("row_max_wide", [P, Q])
        row_max = sb("row_max", [P, Q])
        exp_bias = [sb(f"exp_bias{i}", [P, 1]) for i in range(2)]
        weights = [sb(f"weights{i}", [P, TILES]) for i in range(2)]
        weights_by_row = [sb(f"weights_by_row{i}", [P, TILES, ROWS]) for i in range(2)]
        weighted = [sb(f"weighted{i}", [P, DIRECT * E]) for i in range(2)]
        weight_sums = sb("weight_sums", [P, CHUNKS, 2])
        pooled4 = sb("pooled4", [P, P])
        pooled_t = sb("pooled_t", [P, B])
        cand = sb("cand", [P, NB, E])
        cand_t = sb("cand_t", [P, B])
        first_sb = sb("first_sb", [P, sum(FIRST_COLS.values())])
        later_sb = sb("later_sb", [P, sum(LATER_COLS.values())])

        def part_of(tile, cols, name):
            names = list(cols)
            at = sum(cols[n] for n in names[:names.index(name)])
            return tile[:, at:at + cols[name]]

        ident, row_mask, fold, row_first, same_row, w_b, w_c, b1, f2, b2 = (
            part_of(first_sb, FIRST_COLS, n) for n in FIRST_COLS)
        w_mlp, b_mlp, w_out, b_out = (part_of(later_sb, LATER_COLS, n) for n in LATER_COLS)
        w_mlp = w_mlp.rearrange("p (n h) -> p n h", n=2)
        w_hi = sb("w_hi", [P, H], F32R)
        w_lo = sb("w_lo", [P, H], F32R)
        f2_col = sb("f2_col", [P, 2 * Q])
        ones = sb("ones", [P, P])
        neg_bias = sb("neg_bias", [P, B])
        neg_f2 = sb("neg_f2", [P, 1])
        bias_f2 = sb("bias_f2", [P, B])
        shift_sel = sb("shift_sel", [P, CHUNKS, ROWS])
        shift = sb("shift", [P, CHUNKS])
        sums = sb("sums", [P, CHUNKS])
        inv_sums = sb("inv_sums", [P, CHUNKS])
        inv_sel = sb("inv_sel", [P, CHUNKS, ROWS])
        pooled_n = sb("pooled_n", [P, B])
        z_all = sb("z_all", [P, 2, B])
        logit = sb("logit", [1, B])

        xt_ps = [ctx.enter_context(nc.psum_tensor(f"xt_ps{i}", [P, 512], F32)) for i in range(T_BANKS)]
        z_ps = [ctx.enter_context(nc.psum_tensor(f"z_ps{i}", [P, 512], F32)) for i in range(Z_BANKS)]
        s_ps = ctx.enter_context(nc.psum_tensor("s_ps", [P, 512], F32))
        u_ps = ctx.enter_context(nc.psum_tensor("u_ps", [P, 512], F32))

        x_piece = [sem(f"x_piece{i}") for i in range(2)]
        x_loaded = [sem(f"x_loaded{i}") for i in range(X_BUFS)]
        x_rest_loaded = [sem(f"x_rest_loaded{i}") for i in range(X_BUFS)]
        first_loaded = sem("first_loaded")
        cand_loaded = sem("cand_loaded")
        later_loaded = sem("later_loaded")
        consts_made = sem("consts_made")
        w_hi_made = sem("w_hi_made")
        w_lo_made = sem("w_lo_made")
        cand_t_done = sem("cand_t_done")
        cand_t_copied = sem("cand_t_copied")
        bias_done = sem("bias_done")
        setup_step = sem("setup_step")
        neg_f2_made = sem("neg_f2_made")
        bias_f2_made = sem("bias_f2_made")
        shift_done = sem("shift_done")
        shift_made = sem("shift_made")
        transposed = sem("transposed")
        xh_made = sem("xh_made")
        xl_made = sem("xl_made")
        z_done = sem("z_done")
        hidden_made = sem("hidden_made")
        scores_done = sem("scores_done")
        softmax_step = sem("softmax_step")
        weights_made = sem("weights_made")
        scalar_weighted = sem("scalar_weighted")
        pool_step = sem("pool_step")
        u_free = sem("u_free")
        pooled_done = sem("pooled_done")
        pooled4_copied = sem("pooled4_copied")
        pooled_t_done = sem("pooled_t_done")
        mlp_step = sem("mlp_step")
        row_sums_done = sem("row_sums_done")
        inv_done = sem("inv_done")
        z_all_done = sem("z_all_done")
        z_all_relu = sem("z_all_relu")
        logit_done = sem("logit_done")
        logit_made = sem("logit_made")
        stored = sem("stored")

        SOFTMAX_STEPS = 7
        POOL_STEPS = 7
        OFFLOADED = CHUNKS - 2

        FIRST = 3

        def periods(eng, body):
            for c in range(FIRST):
                body(c, c % X_BUFS, c)
            with eng.Fori(0, (CHUNKS - FIRST - 1) // X_BUFS) as turn:
                for j in range(FIRST, FIRST + X_BUFS):
                    body(turn * X_BUFS + j, j % X_BUFS, FIRST)
            body(CHUNKS - 1, (CHUNKS - 1) % X_BUFS, CHUNKS - 1)

        def hidden_view(buf, k):
            return hidden[buf][:, STARTS[k]:STARTS[k] + GROUPS[k], :].rearrange("p t (b s) -> p t b s", s=PARTS)

        def score_runs(buf):
            return scores[buf][:, :].rearrange("p (t r) -> p r t", r=Q)[:, 0:2, :]

        block = ctx.enter_context(nc.Block())

        @block.sync
        def _(sp):
            cuts = [0, STARTS[1] * E, STARTS[3] * E, DIRECT * E, TILES * E]
            for arrived, a, b in zip([*x_piece, x_loaded[0], x_rest_loaded[0]], cuts[:-1], cuts[1:]):
                sp.dma_start(x[0][:, a:b], behavior_v[0, :, a:b]).then_inc(arrived, 16)
            cut = DIRECT * E
            for c in range(1, X_BUFS):
                sp.dma_start(x[c][:, 0:cut], behavior_v[c, :, 0:cut]).then_inc(x_loaded[c], 16)
                sp.dma_start(x[c][:, cut:], behavior_v[c, :, cut:]).then_inc(x_rest_loaded[c], 16)
            with sp.Fori(0, CHUNKS // X_BUFS - 1) as turn:
                for j in range(X_BUFS):
                    c = turn * X_BUFS + (X_BUFS + j)
                    sp.wait_ge(scalar_weighted, (c + (1 - X_BUFS)) * BY_SCALAR)
                    sp.wait_ge(pool_step, (c - X_BUFS) * POOL_STEPS + 2)
                    sp.dma_start(x[j][:, 0:cut], behavior_v[c, :, 0:cut]).then_inc(x_loaded[j], 16)
                    sp.wait_ge(pooled_done, c + (1 - X_BUFS))
                    sp.dma_start(x[j][:, cut:], behavior_v[c, :, cut:]).then_inc(x_rest_loaded[j], 16)
            sp.wait_ge(logit_made, 1)
            sp.dma_start(out_v, logit[:, :]).then_inc(stored, 16)
            sp.wait_ge(stored, 16)

        @block.gpsimd
        def _(pool):
            nc.gpsimd.memset(ones[:, :], 1.0).then_inc(consts_made, 1)
            pool.wait_ge(first_loaded, 16)

            def mask_weights(c, buf, a):
                n = TILES - a
                pool.wait_ge(weights_made, c * 2 + 2)
                if not (isinstance(c, int) and c == 0):
                    pool.wait_ge(u_free, c)
                nc.gpsimd.tensor_tensor(
                    weights_by_row[buf][:, a:TILES, :],
                    weights[buf][:, a:TILES].unsqueeze(2).to_broadcast([P, n, ROWS]),
                    row_mask.unsqueeze(1).to_broadcast([P, n, ROWS]), ALU.mult).then_inc(pool_step, 1)

            def weight_rows(c, q):
                done = c * POOL_STEPS
                tiles = weighted[q % 2]
                mask_weights(c, q % 2, DIRECT)
                nc.gpsimd.tensor_tensor(
                    tiles[:, BY_SCALAR * E:DIRECT * E].rearrange("p (t e) -> p t e", e=E),
                    x[q][:, BY_SCALAR * E:DIRECT * E].rearrange("p (t e) -> p t e", e=E),
                    weights[q % 2][:, BY_SCALAR:DIRECT].unsqueeze(2).to_broadcast([P, BY_POOL, E]),
                    ALU.mult).then_inc(pool_step, 1)

                def add(to, of, n):
                    nc.gpsimd.tensor_tensor(tiles[:, to * E:(to + n) * E], tiles[:, to * E:(to + n) * E],
                                            tiles[:, of * E:(of + n) * E], ALU.add).then_inc(pool_step, 1)

                pool.wait_ge(pool_step, done + 2)
                add(BY_SCALAR, BY_SCALAR + 4, 4)
                pool.wait_ge(pool_step, done + 3)
                add(BY_SCALAR, BY_SCALAR + 8, 1)
                pool.wait_ge(scalar_weighted, c * BY_SCALAR + 8)
                add(0, 4, 4)
                pool.wait_ge(pool_step, done + 5)
                add(0, BY_SCALAR, 4)
                pool.wait_ge(scalar_weighted, c * BY_SCALAR + BY_SCALAR)
                pool.wait_ge(pool_step, done + 6)
                add(0, 8, 4)

            for c in range(2):
                weight_rows(c, c)
            with pool.Fori(0, (OFFLOADED - 2) // X_BUFS) as turn:
                for j in range(2, 2 + X_BUFS):
                    weight_rows(turn * X_BUFS + j, j % X_BUFS)
            for c in range(OFFLOADED, CHUNKS):
                mask_weights(c, c % 2, 0)

        @block.scalar
        def _(act):
            act.dma_start(first_sb[:, :], first).then_inc(first_loaded, 16)
            act.dma_start(cand[:, :, :], candidate.rearrange("(n p) e -> p n e", p=P)).then_inc(cand_loaded, 16)
            act.dma_start(later_sb[:, :], later).then_inc(later_loaded, 16)
            act.wait_ge(first_loaded, 16)
            nc.scalar.copy(w_hi[:, :], w_b).then_inc(w_hi_made, 1)
            nc.scalar.mul(neg_f2[:, :], f2, -1.0).then_inc(neg_f2_made, 1)
            act.wait_ge(cand_t_done, 1)
            nc.scalar.copy(cand_t[:, :], s_ps[:, :]).then_inc(cand_t_copied, 1)

            def high_half(c, q, k, early):
                w = GROUPS[k] * P
                act.wait_ge(transposed, c * NG + (k + 1))
                if not early:
                    act.wait_ge(z_done, c * NG + (k + 1 - back(q, k, SPLIT_BUFS)))
                nc.scalar.copy(xh[slot(q, k, SPLIT_BUFS)][:, 0:w],
                               xt_ps[slot(q, k, T_BANKS)][:, 0:w]).then_inc(xh_made, 1)

            def exponents(c, buf, early):
                act.wait_ge(softmax_step, c * SOFTMAX_STEPS + SOFTMAX_STEPS)
                if not early:
                    act.wait_ge(pool_step, (c - 2) * POOL_STEPS + 2)
                runs = score_runs(buf)
                nc.scalar.activation(weights[buf][:, 0:RUN], runs[:, 0, :], ACT.Exp, bias=exp_bias[buf][:, :],
                                     accum_out=weight_sums[:, c, 0:1]).then_inc(weights_made, 1)
                skip = 2 * RUN - TILES
                nc.scalar.activation(weights[buf][:, RUN:TILES], runs[:, 1, skip:RUN], ACT.Exp,
                                     bias=exp_bias[buf][:, :],
                                     accum_out=weight_sums[:, c, 1:2]).then_inc(weights_made, 1)

            def weight_tiles(c, q, a, b):
                if a == 0 and b > 0:
                    act.wait_ge(weights_made, c * 2 + 2)
                    if not (isinstance(c, int) and c == 0):
                        act.wait_ge(u_free, c)
                for t in range(a, b):
                    nc.scalar.mul(weighted[q % 2][:, t * E:(t + 1) * E], x[q][:, t * E:(t + 1) * E],
                                  weights[q % 2][:, t:t + 1]).then_inc(scalar_weighted, 1)

            def copy_pooled4(c):
                act.wait_ge(pooled_done, c + 1)
                nc.scalar.copy(pooled4[:, :], u_ps[:, 0:P]).then_inc(pooled4_copied, 1)

            def copy_pooled_t(c):
                act.wait_ge(pooled_t_done, c + 1)
                nc.scalar.copy(pooled_t[:, bass.ds(c * ROWS, ROWS)], u_ps[:, P:P + ROWS]).then_inc(u_free, 1)

            def bias_times_f2():
                act.wait_ge(setup_step, 2)
                act.wait_ge(neg_f2_made, 1)
                nc.scalar.mul(bias_f2[:, :], neg_bias[:, :], neg_f2[:, :]).then_inc(bias_f2_made, 1)

            def relu(part):
                a, b = PART_CHUNKS[part]
                for m in range(2):
                    act.wait_ge(z_all_done, 2 * part + m + 1)
                    nc.scalar.activation(z_all[:, m, a * ROWS:b * ROWS], z_ps[m][:, 0:(b - a) * ROWS], ACT.Relu,
                                         bias=b_mlp[:, m:m + 1]).then_inc(z_all_relu, 1)

            for k in range(AHEAD):
                high_half(0, 0, k, True)
            bias_times_f2()

            def period(c, q, phase):
                for k in range(NG):
                    if k + AHEAD < NG:
                        high_half(c, q, k + AHEAD, phase == 0 and k + AHEAD < SPLIT_BUFS)
                    elif phase != CHUNKS - 1:
                        high_half(c + 1, (q + 1) % X_BUFS, k + AHEAD - NG, False)
                    if k == 1 and phase >= 3:
                        copy_pooled4(c - 3)
                    if k == 4 and phase >= 3:
                        copy_pooled_t(c - 3)
                    if phase >= 2:
                        weight_tiles(c - 2, (q + 2) % X_BUFS, sum(SCALAR_TILES[:k]), sum(SCALAR_TILES[:k + 1]))
                    if k == 5 and phase >= 1:
                        exponents(c - 1, (q + 1) % 2, phase <= 2)

            periods(act, period)
            copy_pooled4(CHUNKS - 3)
            copy_pooled_t(CHUNKS - 3)
            exponents(CHUNKS - 1, (CHUNKS - 1) % 2, False)
            copy_pooled4(CHUNKS - 2)
            relu(0)
            copy_pooled_t(CHUNKS - 2)
            copy_pooled4(CHUNKS - 1)
            copy_pooled_t(CHUNKS - 1)
            relu(1)

        @block.vector
        def _(dve):
            nc.vector.memset(f2_col[:, :], 0.0).then_inc(setup_step, 1)
            nc.vector.memset(part_max[:, :], 0.0).then_inc(consts_made, 1)
            dve.wait_ge(first_loaded, 16)
            dve.wait_ge(setup_step, 1)
            nc.vector.tensor_copy(f2_col[:, Q:Q + 1], f2).then_inc(consts_made, 1)
            dve.wait_ge(w_hi_made, 1)
            nc.vector.tensor_tensor(w_lo[:, :], w_b, w_hi[:, :].bitcast(F32), ALU.subtract).then_inc(w_lo_made, 1)
            dve.wait_ge(bias_done, 1)
            nc.vector.tensor_scalar(neg_bias[:, :], z_ps[2][:, :], b1, -1.0, ALU.add, ALU.mult).then_inc(setup_step, 1)
            dve.wait_ge(setup_step, 2)

            def shifts():
                dve.wait_ge(shift_done, 1)
                nc.vector.tensor_tensor(shift_sel[:, :, :], u_ps[:, :].rearrange("p (c r) -> p c r", r=ROWS),
                                        row_mask.unsqueeze(1).to_broadcast([P, CHUNKS, ROWS]), ALU.mult).then_inc(setup_step, 1)
                dve.wait_ge(setup_step, 3)
                nc.vector.reduce_sum(shift[:, :], shift_sel[:, :, :], axis=AX.X).then_inc(setup_step, 1)
                nc.vector.memset(u_ps[:, 0:P], 0.0).then_inc(u_free, 1)
                dve.wait_ge(setup_step, 4)
                nc.vector.tensor_scalar(shift[:, :], shift[:, :], b2, None, ALU.add).then_inc(shift_made, 1)

            def low_half(c, q, k):
                w = GROUPS[k] * P
                h = xh[slot(q, k, SPLIT_BUFS)][:, 0:w]
                dve.wait_ge(xh_made, c * NG + (k + 1))
                nc.vector.tensor_tensor(xl[slot(q, k, SPLIT_BUFS)][:, 0:w], xt_ps[slot(q, k, T_BANKS)][:, 0:w],
                                        h.bitcast(F32), ALU.subtract).then_inc(xl_made, 1)

            def biased_max(c, q, k, early):
                t = GROUPS[k]
                dve.wait_ge(z_done, c * NG + (k + 1))
                if k == 0 and not early:
                    dve.wait_ge(scores_done, c - 1)
                z = z_ps[slot(q, k, Z_BANKS)][:, 0:t * P].rearrange("p (t b s) -> p t b s", b=ROWS, s=PARTS)
                nb = neg_bias[:, bass.ds(c * ROWS, ROWS)].unsqueeze(1).unsqueeze(3)
                nc.vector.tensor_tensor(hidden_view(q % 2, k), z, nb.to_broadcast([P, t, ROWS, PARTS]),
                                        ALU.max).then_inc(hidden_made, 1)

            def softmax(c, buf, step, early):
                done = c * SOFTMAX_STEPS + step
                if step == 0:
                    dve.wait_ge(scores_done, c + 1)
                    if not early:
                        dve.wait_ge(weights_made, c * 2 - 2)
                    op = nc.vector.transpose(scores[buf][:, :], s_ps[:, 0:RUN * Q])
                else:
                    dve.wait_ge(softmax_step, done)
                if step == 1:
                    op = nc.vector.tensor_reduce(part_max[:, 0:1], score_runs(buf), axis=AX.XY, op=ALU.max)
                if step == 2:
                    op = nc.vector.transpose(part_max_t[:, :], part_max[:, :])
                if step == 3:
                    op = nc.vector.tensor_reduce(row_max_t[:, :], part_max_t[:, :].rearrange("p (b s) -> p b s", s=PARTS),
                                                 axis=AX.X, op=ALU.max)
                if step == 4:
                    op = nc.vector.tensor_copy(row_max_wide[:, :].rearrange("p (b s) -> p b s", s=PARTS),
                                               row_max_t[:, :].unsqueeze(2).to_broadcast([P, Q // PARTS, PARTS]))
                if step == 5:
                    op = nc.vector.transpose(row_max[:, :], row_max_wide[:, :])
                if step == 6:
                    own = shift[:, bass.ds(c, 1)]
                    op = nc.vector.scalar_tensor_tensor(exp_bias[buf][:, :], row_max[:, 0:1], own, own,
                                                        ALU.add, ALU.subtract, reverse1=True)
                op.then_inc(softmax_step, 1)

            def inverses(part, row_sums, step):
                a, b = PART_CHUNKS[part]
                if step == 0:
                    dve.wait_ge(weights_made, 2 * b)
                    op = nc.vector.tensor_tensor(sums[:, a:b], weight_sums[:, a:b, 0], weight_sums[:, a:b, 1], ALU.add)
                if step == 1:
                    dve.wait_ge(row_sums_done, part + 1)
                    op = nc.vector.reciprocal(inv_sums[:, a:b], row_sums[:, 0:b - a])
                if step == 2:
                    dve.wait_ge(mlp_step, 4 * part + 2)
                    op = nc.vector.tensor_tensor(
                        inv_sel[:, a:b, :], inv_sums[:, a:b].unsqueeze(2).to_broadcast([P, b - a, ROWS]),
                        row_first.unsqueeze(1).to_broadcast([P, b - a, ROWS]), ALU.mult)
                op.then_inc(mlp_step, 1)

            def normalise(part, inv):
                a, b = PART_CHUNKS[part]
                dve.wait_ge(inv_done, part + 1)
                dve.wait_ge(u_free, b + 1)
                nc.vector.tensor_tensor(pooled_n[:, a * ROWS:b * ROWS], inv[:, 0:(b - a) * ROWS],
                                        pooled_t[:, a * ROWS:b * ROWS], ALU.mult).then_inc(mlp_step, 1)

            for k in range(LOW_AHEAD):
                low_half(0, 0, k)

            def period(c, q, phase):
                for k in range(NG):
                    if k + LOW_AHEAD < NG:
                        low_half(c, q, k + LOW_AHEAD)
                    elif phase != CHUNKS - 1:
                        low_half(c + 1, (q + 1) % X_BUFS, k + LOW_AHEAD - NG)
                    if phase >= 1 and 1 <= k <= 4:
                        softmax(c - 1, (q + 1) % 2, 2 * (k - 1), phase <= 2)
                    biased_max(c, q, k, phase < 2)
                    if phase >= 1 and 1 <= k <= 3:
                        softmax(c - 1, (q + 1) % 2, 2 * (k - 1) + 1, phase <= 2)
                    if phase == 0 and k == 3:
                        shifts()
                    if phase == CHUNKS - 1 and k in (2, 4, 5):
                        inverses(0, s_ps, {2: 0, 4: 1, 5: 2}[k])
                if phase == CHUNKS - 1:
                    normalise(0, s_ps)

            periods(dve, period)
            last = CHUNKS - 1
            for step in range(SOFTMAX_STEPS):
                softmax(last, last % 2, step, False)
            for step in range(3):
                inverses(1, xt_ps[1], step)
            normalise(1, xt_ps[2])
            dve.wait_ge(logit_done, 1)
            nc.vector.tensor_scalar(logit[:, :], xt_ps[0][0:1, :], b_out[0:1, :], None, ALU.add).then_inc(logit_made, 1)

        @block.tensor
        def _(pe):
            def transpose(c, q, k, loaded, early):
                if loaded is not None:
                    pe.wait_ge(loaded[0], loaded[1])
                if not early:
                    pe.wait_ge(xl_made, c * NG + (k + 1 - back(q, k, T_BANKS)))
                for j in range(GROUPS[k]):
                    t = STARTS[k] + j
                    op = nc.tensor.transpose(xt_ps[slot(q, k, T_BANKS)][:, j * P:(j + 1) * P],
                                             x[q][:, t * E:(t + 1) * E], ident)
                op.then_inc(transposed, 1)

            def products(c, q, k, early):
                w = GROUPS[k] * P
                s = slot(q, k, SPLIT_BUFS)
                z = z_ps[slot(q, k, Z_BANKS)][:, 0:w]
                pe.wait_ge(xl_made, c * NG + (k + 1))
                if not early:
                    pe.wait_ge(hidden_made, c * NG + (k + 1 - back(q, k, Z_BANKS)))
                nc.tensor.matmul(z, w_hi[:, :], xh[s][:, 0:w], start=True, stop=False)
                nc.tensor.matmul(z, w_lo[:, :], xh[s][:, 0:w], start=False, stop=False)
                nc.tensor.matmul(z, w_hi[:, :], xl[s][:, 0:w], start=False, stop=True).then_inc(z_done, 1)

            def score(c, buf, r, first):
                pe.wait_ge(hidden_made, c * NG + (NG if r == 1 else FIRST_RUN_GROUPS))
                if r == 0 and not first:
                    pe.wait_ge(softmax_step, c * SOFTMAX_STEPS - (SOFTMAX_STEPS - 1))
                for g in range(P // Q):
                    op = nc.tensor.matmul(
                        s_ps[g * Q:(g + 1) * Q, 0:RUN * Q].rearrange("p (t s) -> p t s", s=Q),
                        f2_col[:, Q - r:2 * Q - r],
                        hidden[buf][:, RUN_START[r]:RUN_START[r] + RUN, g * Q:(g + 1) * Q],
                        start=(r == 0), stop=(r == 1), tile_position=(0, g * Q))
                if r == 1:
                    op.then_inc(scores_done, 1)

            def sum_tile(g, weights_ap, rows_ap, start, stop):
                return nc.tensor.matmul(u_ps[g * Q:g * Q + ROWS, 0:P], weights_ap, rows_ap,
                                        start=start, stop=stop, tile_position=(0, g * Q))

            def weighted_sum(c, q):
                pe.wait_ge(pool_step, c * POOL_STEPS + POOL_STEPS)
                pe.wait_ge(u_free, c + 1)
                for g in range(SUMMED):
                    t = DIRECT + g
                    sum_tile(g, weights_by_row[q % 2][:, t, :], x[q][:, t * E:(t + 1) * E], True, False)
                for g in range(SUMMED):
                    op = sum_tile(g, row_mask, weighted[q % 2][:, g * E:(g + 1) * E], False, True)
                op.then_inc(pooled_done, 1)

            def weighted_sum_alone(c):
                pe.wait_ge(pool_step, OFFLOADED * POOL_STEPS + (c - OFFLOADED + 1))
                pe.wait_ge(u_free, c + 1)
                for t in range(TILES):
                    op = sum_tile(t % SUMMED, weights_by_row[c % 2][:, t, :],
                                  x[c % X_BUFS][:, t * E:(t + 1) * E], t < SUMMED, t >= TILES - SUMMED)
                op.then_inc(pooled_done, 1)

            def transpose_sums(c):
                pe.wait_ge(pooled4_copied, c + 1)
                nc.tensor.matmul(u_ps[:, P:P + ROWS], pooled4[:, :], fold, start=True, stop=True).then_inc(pooled_t_done, 1)

            def shift_sums():
                pe.wait_ge(consts_made, 3)
                pe.wait_ge(bias_f2_made, 1)
                nc.tensor.matmul(u_ps[:, :], ones[:, :], bias_f2[:, :], start=True, stop=True).then_inc(shift_done, 1)

            def row_sums(part, bank):
                a, b = PART_CHUNKS[part]
                pe.wait_ge(mlp_step, 4 * part + 1)
                nc.tensor.matmul(bank[:, 0:b - a], same_row, sums[:, a:b], start=True, stop=True).then_inc(row_sums_done, 1)

            def spread_inverses(part, bank):
                a, b = PART_CHUNKS[part]
                pe.wait_ge(mlp_step, 4 * part + 3)
                nc.tensor.matmul(bank[:, 0:(b - a) * ROWS], ones[:, :],
                                 inv_sel[:, a:b, :].rearrange("p c r -> p (c r)"),
                                 start=True, stop=True).then_inc(inv_done, 1)

            def mlp(part):
                a, b = (n * ROWS for n in PART_CHUNKS[part])
                if part == 0:
                    pe.wait_ge(later_loaded, 16)
                    pe.wait_ge(hidden_made, CHUNKS * NG)
                else:
                    pe.wait_ge(z_all_relu, 2)
                for m in range(2):
                    nc.tensor.matmul(z_ps[m][:, 0:b - a], w_mlp[:, 1, m * P:(m + 1) * P], cand_t[:, a:b],
                                     start=True, stop=False)
                pe.wait_ge(mlp_step, 4 * part + 4)
                for m in range(2):
                    nc.tensor.matmul(z_ps[m][:, 0:b - a], w_mlp[:, 0, m * P:(m + 1) * P], pooled_n[:, a:b],
                                     start=False, stop=True).then_inc(z_all_done, 1)

            def logits(part):
                a, b = (n * ROWS for n in PART_CHUNKS[part])
                for m in range(2):
                    pe.wait_ge(z_all_relu, 2 * part + m + 1)
                    op = nc.tensor.matmul(xt_ps[0][0:1, a:b], w_out[:, m:m + 1], z_all[:, m, a:b],
                                          start=(m == 0), stop=(m == 1))
                if part == 1:
                    op.then_inc(logit_done, 1)

            pe.wait_ge(first_loaded, 16)
            pe.wait_ge(cand_loaded, 16)
            for n in range(NB):
                op = nc.tensor.transpose(s_ps[:, n * P:(n + 1) * P], cand[:, n, :], ident)
            op.then_inc(cand_t_done, 1)
            transpose(0, 0, 0, (x_piece[0], 16), True)
            pe.wait_ge(cand_t_copied, 1)
            nc.tensor.matmul(z_ps[2][:, :], w_c, cand_t[:, :], start=True, stop=True).then_inc(bias_done, 1)
            transpose(0, 0, 1, (x_piece[1], 16), True)
            transpose(0, 0, 2, None, True)
            pe.wait_ge(w_lo_made, 1)

            def loads(c, q):
                return (c + (X_BUFS - q)) * (16 // X_BUFS)

            def period(c, q, phase):
                for k in range(NG):
                    products(c, q, k, phase == 0 and k < Z_BANKS)
                    if k + AHEAD < NG:
                        arrived = None
                        if phase == 0 and k == 0:
                            arrived = (x_loaded[0], 16)
                        if k + AHEAD == 5:
                            arrived = (x_rest_loaded[q], loads(c, q))
                        transpose(c, q, k + AHEAD, arrived, False)
                    elif phase != CHUNKS - 1:
                        nq = (q + 1) % X_BUFS
                        transpose(c + 1, nq, k + AHEAD - NG,
                                  (x_loaded[nq], loads(c + 1, nq)) if k == NG - AHEAD else None, False)
                    if k == 0 and phase >= 3:
                        weighted_sum(c - 3, (q + 1) % X_BUFS)
                    if k == 0 and phase >= 1:
                        score(c - 1, (q + 1) % 2, 1, False)
                    if k == 5 and phase != CHUNKS - 1:
                        score(c, q % 2, 0, phase == 0)
                    if k == 3 and phase >= 3:
                        transpose_sums(c - 3)
                    if phase == 0 and k == 1:
                        shift_sums()
                    if phase == CHUNKS - 1 and k == 3:
                        row_sums(0, s_ps)
                    if phase == CHUNKS - 1 and k == 6:
                        spread_inverses(0, s_ps)

            periods(pe, period)
            last = CHUNKS - 1
            pe.wait_ge(mlp_step, 4)
            score(last, last % 2, 0, False)
            score(last, last % 2, 1, False)
            weighted_sum(last - 2, (last - 2) % X_BUFS)
            transpose_sums(last - 2)
            weighted_sum_alone(last - 1)
            mlp(0)
            transpose_sums(last - 1)
            logits(0)
            row_sums(1, xt_ps[1])
            spread_inverses(1, xt_ps[2])
            weighted_sum_alone(last)
            transpose_sums(last)
            mlp(1)
            logits(1)


def layout_constants():
    import numpy as np

    p = np.arange(P)[:, None]
    rows = np.arange(P // PARTS)[None, :]
    row_mask = p // PARTS == rows
    each = [p == p.T, row_mask, p % Q == rows, row_mask & (p % PARTS == 0), p // PARTS == p.T // PARTS]
    return [m.astype(np.float32) for m in each]


def kernel(r_behavior_emb, r_candidate_emb, L0_rec_fc1_w, L0_rec_fc1_b, L0_rec_fc2_w, L0_rec_fc2_b,
           L0_rec_mlp1_w, L0_rec_mlp1_b, L0_rec_mlp2_w, L0_rec_mlp2_b):
    import numpy as np
    import concourse.bacc as bacc
    from concourse.bass_utils import run_bass_kernel_spmd

    def column(v):
        v = np.asarray(v).reshape(-1)
        return np.broadcast_to(v, (P, 1)) if v.size == 1 else v.reshape(-1, P).T

    fc1_w, mlp1_w = np.asarray(L0_rec_fc1_w), np.asarray(L0_rec_mlp1_w)
    first = np.concatenate([*layout_constants(), fc1_w[:P], fc1_w[P:], column(L0_rec_fc1_b),
                            column(L0_rec_fc2_w), column(L0_rec_fc2_b)], axis=1)
    later = np.concatenate([mlp1_w[:P], mlp1_w[P:], column(L0_rec_mlp1_b), column(L0_rec_mlp2_w),
                            column(L0_rec_mlp2_b)], axis=1)
    arrays = {"behavior": r_behavior_emb, "candidate": r_candidate_emb, "first": first, "later": later}
    arrays = {f"in_{name}": np.ascontiguousarray(a) for name, a in arrays.items()}
    nc = bacc.Bacc("TRN2", target_bir_lowering=False, num_devices=1)
    args = [nc.dram_tensor(name, a.shape, mybir.dt.from_np(a.dtype), kind="ExternalInput").ap()
            for name, a in arrays.items()]
    args.append(nc.dram_tensor("out_logit", (r_behavior_emb.shape[0],), F32, kind="ExternalOutput").ap())
    attention_pooling_kernel(nc, *args)
    r = run_bass_kernel_spmd(nc, [arrays], core_ids=[0])
    return r.results[0]["out_logit"]
```

```python
from contextlib import ExitStack

import concourse.bass as bass
from concourse import mybir

F32 = mybir.dt.float32
F32R = mybir.dt.float32r
ALU = mybir.AluOpType
ACT = mybir.ActivationFunctionType
AX = mybir.AxisListType

P = 128
PARTS = 8
GROUPS = [4, 4, 4, 4, 3, 3, 3]
NG = len(GROUPS)
STARTS = [sum(GROUPS[:k]) for k in range(NG)]
X_BUFS = 4
SCALAR_TILES = [5, 2, 2, 1, 1, 1, 0]
BY_SCALAR = sum(SCALAR_TILES)
BY_POOL = 9
SUMMED = 4
SPLIT_BUFS = 4
Z_BANKS = 3
Z_SHORT = (1, 27)
T_SHORT = (5, 7)
T_BANKS = 3
Q = 32
PIECES = 3
WARM_UP = 7
AHEAD = 3
LOW_AHEAD = 2
TAIL = 4


def rotation(n, short):
    count = X_BUFS * NG
    slots = list(range(n))
    for g in range(n, 2 * count):
        by_age = sorted(range(n), key=lambda b: max(i for i, used in enumerate(slots) if used == b))
        slots.append(by_age[1 if g % count in short else 0])
    assert slots[:count] == slots[count:]
    used = [next(d for d in range(1, count) if slots[count + g - d] == slots[g]) for g in range(count)]
    return slots[:count], used


ROTATION = {"split": rotation(SPLIT_BUFS, ()), "z": rotation(Z_BANKS, Z_SHORT), "xt": rotation(T_BANKS, T_SHORT)}


def slot(q, k, buffers):
    return ROTATION[buffers][0][q * NG + k]


def back(q, k, buffers):
    return ROTATION[buffers][1][q * NG + k]


FIRST_COLS = {"ident": P, "row_mask": 3 * P // PARTS, "fold": Q, "row_first": P // PARTS, "own_row": Q // PARTS, "same_row": P,
              "w_b": P, "w_c": P, "b1": 1, "f2": 1, "b2": 1}
LATER_COLS = {"w_mlp": 4 * P, "b_mlp": 2, "w_out": 2, "b_out": 1}


def attention_pooling_kernel(nc, behavior, candidate, first, later, out):
    B, S, E = behavior.shape
    H = P
    assert E == P and S % PARTS == 0
    TILES = S // PARTS
    ROWS = P // PARTS
    CHUNKS = B // ROWS
    NB = B // P
    assert sum(GROUPS) == TILES and CHUNKS % X_BUFS == 0 and X_BUFS == 4
    RUN = (TILES + 1) // 2
    FIRST_RUN_GROUPS = next(k for k in range(NG) if STARTS[k] >= RUN)
    PART_CHUNKS = [(0, CHUNKS - TAIL), (CHUNKS - TAIL, CHUNKS)]
    CAND_PARTS = [(0, 1), (1, NB)]
    DIRECT = BY_SCALAR + BY_POOL
    assert TILES - DIRECT == SUMMED == P // Q and STARTS[5] < DIRECT < STARTS[6]

    behavior_v = behavior.rearrange("(c r) (a t) e -> c (r a) (t e)", r=ROWS, a=PARTS)

    with ExitStack() as ctx:
        def sb(name, shape, dt=F32):
            return ctx.enter_context(nc.sbuf_tensor(name, shape, dt))

        def sem(name):
            return ctx.enter_context(nc.semaphore(name))

        x = [sb(f"x{i}", [P, TILES * E]) for i in range(X_BUFS)]
        xh = [sb(f"xh{i}", [P, 4 * P], F32R) for i in range(SPLIT_BUFS)]
        xl = [sb(f"xl{i}", [P, 4 * P], F32R) for i in range(SPLIT_BUFS)]
        hidden = [sb(f"hidden{i}", [P, TILES, P]) for i in range(2)]
        scores = [sb(f"scores{i}", [P, RUN * Q]) for i in range(2)]
        part_max = sb("part_max", [P, Q])
        part_max_t = sb("part_max_t", [P, Q])
        row_max_t = sb("row_max_t", [P, Q // PARTS])
        row_max_wide = sb("row_max_wide", [P, Q])
        row_max = sb("row_max", [P, Q])
        exp_bias = [sb(f"exp_bias{i}", [P, 1]) for i in range(2)]
        weights = [sb(f"weights{i}", [P, TILES]) for i in range(2)]
        weights_by_row = [sb(f"weights_by_row{i}", [P, TILES, 2 * ROWS]) for i in range(2)]
        weighted = [sb(f"weighted{i}", [P, DIRECT * E]) for i in range(2)]
        weight_sums = sb("weight_sums", [P, CHUNKS, 2])
        pooled4 = sb("pooled4", [P, P])
        pooled_t = sb("pooled_t", [P, B])
        cand = sb("cand", [P, NB, E])
        cand_t = sb("cand_t", [P, B])
        first_sb = sb("first_sb", [P, sum(FIRST_COLS.values())])
        later_sb = sb("later_sb", [P, sum(LATER_COLS.values())])

        def part_of(tile, cols, name):
            names = list(cols)
            at = sum(cols[n] for n in names[:names.index(name)])
            return tile[:, at:at + cols[name]]

        ident, row_mask, fold, row_first, own_row, same_row, w_b, w_c, b1, f2, b2 = (
            part_of(first_sb, FIRST_COLS, n) for n in FIRST_COLS)
        w_mlp, b_mlp, w_out, b_out = (part_of(later_sb, LATER_COLS, n) for n in LATER_COLS)
        w_mlp = w_mlp.rearrange("p (n h) -> p n h", n=2)
        pair_half = [slice(0, ROWS), slice(ROWS, 2 * ROWS)]
        pair_mask = [row_mask[:, ROWS:3 * ROWS], row_mask[:, 0:2 * ROWS]]
        row_mask = row_mask[:, ROWS:2 * ROWS]
        w_hi = sb("w_hi", [P, H], F32R)
        w_lo = sb("w_lo", [P, H], F32R)
        zeros = sb("zeros", [P, Q])
        f2_col = sb("f2_col", [P, Q])
        ones = sb("ones", [P, P])
        neg_bias = sb("neg_bias", [P, B])
        neg_f2 = sb("neg_f2", [P, 1])
        bias_f2 = sb("bias_f2", [P, B])
        shift_sel = sb("shift_sel", [P, CHUNKS, Q // PARTS])
        shift = sb("shift", [P, CHUNKS])
        sums = sb("sums", [P, CHUNKS])
        inv_sums = sb("inv_sums", [P, CHUNKS])
        inv_sel = sb("inv_sel", [P, CHUNKS, ROWS])
        pooled_n = sb("pooled_n", [P, B])
        z_all = sb("z_all", [P, 2, B])
        logit = sb("logit", [P, 2, B // (P // Q)])
        quarter = [(b - a) * ROWS // (P // Q) for a, b in PART_CHUNKS]

        xt_ps = [ctx.enter_context(nc.psum_tensor(f"xt_ps{i}", [P, 512], F32)) for i in range(T_BANKS)]
        z_ps = [ctx.enter_context(nc.psum_tensor(f"z_ps{i}", [P, 512], F32)) for i in range(Z_BANKS)]
        s_ps = ctx.enter_context(nc.psum_tensor("s_ps", [P, 512], F32))
        u_ps = ctx.enter_context(nc.psum_tensor("u_ps", [P, 512], F32))

        last_xt = [slot(X_BUFS - 1, k, "xt") for k in range(NG)]
        last_z = [slot(X_BUFS - 1, k, "z") for k in range(NG)]
        mlp_ps = [[xt_ps[last_xt[4]], xt_ps[last_xt[5]]], [s_ps, u_ps]]
        logit_ps = xt_ps[last_xt[6]]
        inverse_ps = [z_ps[last_z[3]], z_ps[last_z[6]]]
        last_pair_ps = z_ps[last_z[5]]
        assert len(set(last_xt[4:7])) == 3 and last_z[3] not in last_z[4:7] and last_z[5] != last_z[6]

        x_piece = [sem(f"x_piece{i}") for i in range(PIECES)]
        x_loaded = [sem(f"x_loaded{i}") for i in range(X_BUFS)]
        x_rest_loaded = [sem(f"x_rest_loaded{i}") for i in range(X_BUFS)]
        first_loaded = sem("first_loaded")
        cand_loaded = [sem(f"cand_loaded{i}") for i in range(2)]
        later_loaded = sem("later_loaded")
        ones_made = sem("ones_made")
        f2_col_made = sem("f2_col_made")
        part_max_cleared = sem("part_max_cleared")
        w_hi_made = sem("w_hi_made")
        w_lo_made = sem("w_lo_made")
        cand_t_done = sem("cand_t_done")
        cand_t_copied = sem("cand_t_copied")
        bias_done = sem("bias_done")
        setup_step = sem("setup_step")
        neg_f2_made = sem("neg_f2_made")
        bias_f2_made = sem("bias_f2_made")
        shift_done = sem("shift_done")
        shift_made = sem("shift_made")
        transposed = sem("transposed")
        xh_made = sem("xh_made")
        xl_made = sem("xl_made")
        z_done = sem("z_done")
        hidden_made = sem("hidden_made")
        scores_done = sem("scores_done")
        softmax_step = sem("softmax_step")
        weights_made = sem("weights_made")
        scalar_weighted = sem("scalar_weighted")
        rows_cleared = sem("rows_cleared")
        pool_step = sem("pool_step")
        last_masked = sem("last_masked")
        pooled4_copied = sem("pooled4_copied")
        pooled_t_done = sem("pooled_t_done")
        u_free = sem("u_free")
        pooled_done = sem("pooled_done")
        mlp_step = sem("mlp_step")
        row_sums_done = sem("row_sums_done")
        inv_done = sem("inv_done")
        z_all_done = sem("z_all_done")
        z_all_relu = sem("z_all_relu")
        logit_done = sem("logit_done")
        logit_made = sem("logit_made")
        stored = sem("stored")

        SOFTMAX_STEPS = 7
        POOL_STEPS = 7
        OFFLOADED = CHUNKS - 2

        BIAS_STEP, SUM_STEP, SHIFT_STEP = 3, 4, 5
        FIRST = 3

        def periods(eng, body):
            for c in range(FIRST):
                body(c, c % X_BUFS, c)
            with eng.Fori(0, (CHUNKS - FIRST - 1) // X_BUFS) as turn:
                for j in range(FIRST, FIRST + X_BUFS):
                    body(turn * X_BUFS + j, j % X_BUFS, FIRST)
            body(CHUNKS - 1, (CHUNKS - 1) % X_BUFS, CHUNKS - 1)

        def hidden_view(buf, k):
            return hidden[buf][:, STARTS[k]:STARTS[k] + GROUPS[k], :].rearrange("p t (b s) -> p t b s", s=PARTS)

        def score_runs(buf):
            return scores[buf][:, :].rearrange("p (t r) -> p r t", r=Q)[:, 0:2, :]

        block = ctx.enter_context(nc.Block())

        @block.sync
        def _(sp):
            cuts = [0, *(STARTS[k] * E for k in range(1, PIECES + 1)), DIRECT * E, TILES * E]
            arrivals = [*x_piece, x_loaded[0], x_rest_loaded[0]]
            candidate_v = candidate.rearrange("(n p) e -> p n e", p=P)
            for i, arrived in enumerate(arrivals):
                sp.dma_start(x[0][:, cuts[i]:cuts[i + 1]], behavior_v[0, :, cuts[i]:cuts[i + 1]]).then_inc(arrived, 16)
                if i in (0, 2):
                    a, b = CAND_PARTS[i // 2]
                    sp.dma_start(cand[:, a:b, :], candidate_v[:, a:b, :]).then_inc(cand_loaded[i // 2], 16)
            cut = DIRECT * E
            for c in range(1, X_BUFS):
                if c == 2:
                    sp.dma_start(later_sb[:, :], later).then_inc(later_loaded, 16)
                sp.dma_start(x[c][:, 0:cut], behavior_v[c, :, 0:cut]).then_inc(x_loaded[c], 16)
                sp.dma_start(x[c][:, cut:], behavior_v[c, :, cut:]).then_inc(x_rest_loaded[c], 16)
            with sp.Fori(0, CHUNKS // X_BUFS - 1) as turn:
                for j in range(X_BUFS):
                    c = turn * X_BUFS + (X_BUFS + j)
                    sp.wait_ge(scalar_weighted, (c + (1 - X_BUFS)) * BY_SCALAR)
                    sp.wait_ge(pool_step, (c - X_BUFS) * POOL_STEPS + 2)
                    sp.dma_start(x[j][:, 0:cut], behavior_v[c, :, 0:cut]).then_inc(x_loaded[j], 16)
                    sp.wait_ge(pooled_done, c + (2 - X_BUFS))
                    sp.dma_start(x[j][:, cut:], behavior_v[c, :, cut:]).then_inc(x_rest_loaded[j], 16)
            for part, (a, b) in enumerate(PART_CHUNKS):
                sp.wait_ge(logit_made, part + 1)
                sp.dma_start(out[a * ROWS:b * ROWS].rearrange("(g n) -> g n", g=P // Q),
                             logit[0:P:Q, part, 0:quarter[part]]).then_inc(stored, 16)
            sp.wait_ge(stored, 2 * 16)

        @block.gpsimd
        def _(pool):
            nc.gpsimd.memset(ones[:, :], 1.0).then_inc(ones_made, 1)
            for buf in range(2):
                nc.gpsimd.memset(weights_by_row[buf][:, :, :], 0.0).then_inc(rows_cleared, 1)
            pool.wait_ge(rows_cleared, 2)
            pool.wait_ge(first_loaded, 16)

            def mask_weights(c, buf, a):
                n = TILES - a
                pool.wait_ge(weights_made, c * 2 + 2)
                if not (isinstance(c, int) and c == 0):
                    pool.wait_ge(pooled_done, c)
                nc.gpsimd.tensor_tensor(
                    weights_by_row[buf][:, a:TILES, pair_half[buf]],
                    weights[buf][:, a:TILES].unsqueeze(2).to_broadcast([P, n, ROWS]),
                    row_mask.unsqueeze(1).to_broadcast([P, n, ROWS]), ALU.mult).then_inc(pool_step, 1)

            def weight_rows(c, q):
                done = c * POOL_STEPS
                tiles = weighted[q % 2]
                mask_weights(c, q % 2, DIRECT)
                nc.gpsimd.tensor_tensor(
                    tiles[:, BY_SCALAR * E:DIRECT * E].rearrange("p (t e) -> p t e", e=E),
                    x[q][:, BY_SCALAR * E:DIRECT * E].rearrange("p (t e) -> p t e", e=E),
                    weights[q % 2][:, BY_SCALAR:DIRECT].unsqueeze(2).to_broadcast([P, BY_POOL, E]),
                    ALU.mult).then_inc(pool_step, 1)

                def add(to, of, n):
                    nc.gpsimd.tensor_tensor(tiles[:, to * E:(to + n) * E], tiles[:, to * E:(to + n) * E],
                                            tiles[:, of * E:(of + n) * E], ALU.add).then_inc(pool_step, 1)

                pool.wait_ge(pool_step, done + 2)
                add(BY_SCALAR, BY_SCALAR + 4, 4)
                pool.wait_ge(pool_step, done + 3)
                add(BY_SCALAR, BY_SCALAR + 8, 1)
                pool.wait_ge(scalar_weighted, c * BY_SCALAR + 8)
                add(0, 4, 4)
                pool.wait_ge(pool_step, done + 5)
                add(0, BY_SCALAR, 4)
                pool.wait_ge(scalar_weighted, c * BY_SCALAR + BY_SCALAR)
                pool.wait_ge(pool_step, done + 6)
                add(0, 8, 4)

            for c in range(2):
                weight_rows(c, c)
            with pool.Fori(0, (OFFLOADED - 2) // X_BUFS) as turn:
                for j in range(2, 2 + X_BUFS):
                    weight_rows(turn * X_BUFS + j, j % X_BUFS)
            mask_weights(OFFLOADED, OFFLOADED % 2, 0)

        @block.scalar
        def _(act):
            act.dma_start(first_sb[:, :], first).then_inc(first_loaded, 16)
            act.wait_ge(setup_step, 1)
            nc.scalar.copy(part_max[:, :], zeros[:, :]).then_inc(part_max_cleared, 1)
            act.wait_ge(first_loaded, 16)
            nc.scalar.copy(w_hi[:, :], w_b).then_inc(w_hi_made, 1)
            nc.scalar.mul(neg_f2[:, :], f2, -1.0).then_inc(neg_f2_made, 1)

            def copy_candidates(part):
                a, b = CAND_PARTS[part]
                act.wait_ge(cand_t_done, part + 1)
                nc.scalar.copy(cand_t[:, a * P:b * P], s_ps[:, a * P:b * P]).then_inc(cand_t_copied, 1)

            def high_half(c, q, k, early):
                w = GROUPS[k] * P
                act.wait_ge(transposed, c * NG + (k + 1))
                if not early:
                    act.wait_ge(z_done, c * NG + (k + 1 - back(q, k, "split")))
                nc.scalar.copy(xh[slot(q, k, "split")][:, 0:w],
                               xt_ps[slot(q, k, "xt")][:, 0:w]).then_inc(xh_made, 1)

            def exponents(c, buf, early):
                act.wait_ge(softmax_step, c * SOFTMAX_STEPS + SOFTMAX_STEPS)
                if not early:
                    act.wait_ge(pool_step, (c - 2) * POOL_STEPS + 2)
                runs = score_runs(buf)
                nc.scalar.activation(weights[buf][:, 0:RUN], runs[:, 1, :], ACT.Exp, bias=exp_bias[buf][:, :],
                                     accum_out=weight_sums[:, c, 0:1]).then_inc(weights_made, 1)
                nc.scalar.activation(weights[buf][:, RUN:TILES], runs[:, 0, 2 * RUN - TILES:RUN], ACT.Exp,
                                     bias=exp_bias[buf][:, :],
                                     accum_out=weight_sums[:, c, 1:2]).then_inc(weights_made, 1)

            def weight_tiles(c, q, a, b):
                if a == 0 and b > 0:
                    act.wait_ge(weights_made, c * 2 + 2)
                    if not (isinstance(c, int) and c == 0):
                        act.wait_ge(pooled_done, c)
                for t in range(a, b):
                    nc.scalar.mul(weighted[q % 2][:, t * E:(t + 1) * E], x[q][:, t * E:(t + 1) * E],
                                  weights[q % 2][:, t:t + 1]).then_inc(scalar_weighted, 1)

            def copy_pooled4(c, bank):
                act.wait_ge(pooled_done, c + 2)
                nc.scalar.copy(pooled4[:, :], bank[:, 0:P]).then_inc(pooled4_copied, 2)

            def copy_pooled_t(c, bank):
                act.wait_ge(pooled_t_done, c + 1)
                nc.scalar.copy(pooled_t[:, bass.ds((c - 1) * ROWS, 2 * ROWS)],
                               bank[:, P:P + 2 * ROWS]).then_inc(u_free, 2)

            def bias_times_f2():
                act.wait_ge(setup_step, 3)
                act.wait_ge(neg_f2_made, 1)
                nc.scalar.mul(bias_f2[:, :], neg_bias[:, :], neg_f2[:, :]).then_inc(bias_f2_made, 1)

            def relu(part, m):
                a, b = PART_CHUNKS[part]
                act.wait_ge(z_all_done, 2 * part + m + 1)
                nc.scalar.activation(z_all[:, m, a * ROWS:b * ROWS], mlp_ps[part][m][:, 0:(b - a) * ROWS], ACT.Relu,
                                     bias=b_mlp[:, m:m + 1]).then_inc(z_all_relu, 1)

            high_half(0, 0, 0, True)
            copy_candidates(0)
            high_half(0, 0, 1, True)
            high_half(0, 0, 2, True)

            def period(c, q, phase):
                for k in range(NG):
                    if phase == 0 and k == 0:
                        copy_candidates(1)
                    if k + AHEAD < NG:
                        high_half(c, q, k + AHEAD, phase == 0 and k + AHEAD < SPLIT_BUFS)
                    elif phase != CHUNKS - 1:
                        high_half(c + 1, (q + 1) % X_BUFS, k + AHEAD - NG, False)
                    if phase == 0 and k == 2:
                        bias_times_f2()
                    if k == 1 and phase >= 3 and (q - 3) % 2 == 1:
                        copy_pooled4(c - 3, u_ps)
                    if k == 4 and phase >= 3 and (q - 3) % 2 == 1:
                        copy_pooled_t(c - 3, u_ps)
                    if phase >= 2:
                        weight_tiles(c - 2, (q + 2) % X_BUFS, sum(SCALAR_TILES[:k]), sum(SCALAR_TILES[:k + 1]))
                    if k == 5 and phase >= 1:
                        exponents(c - 1, (q + 1) % 2, phase <= 2)

            periods(act, period)
            copy_pooled4(CHUNKS - 3, u_ps)
            copy_pooled_t(CHUNKS - 3, u_ps)
            exponents(CHUNKS - 1, (CHUNKS - 1) % 2, False)
            copy_pooled4(CHUNKS - 1, last_pair_ps)
            relu(0, 0)
            copy_pooled_t(CHUNKS - 1, last_pair_ps)
            relu(0, 1)
            relu(1, 0)
            relu(1, 1)

        @block.vector
        def _(dve):
            nc.vector.memset(zeros[:, :], 0.0).then_inc(setup_step, 1)
            dve.wait_ge(first_loaded, 16)
            dve.wait_ge(setup_step, 1)
            nc.vector.tensor_copy(f2_col[:, 2:Q], zeros[:, 2:Q]).then_inc(f2_col_made, 1)
            nc.vector.tensor_copy(f2_col[:, 0:2], f2.to_broadcast([P, 2])).then_inc(f2_col_made, 1)
            dve.wait_ge(w_hi_made, 1)
            nc.vector.tensor_tensor(w_lo[:, :], w_b, w_hi[:, :].bitcast(F32), ALU.subtract).then_inc(w_lo_made, 1)

            def negative_bias(part):
                a, b = (n * P for n in CAND_PARTS[part])
                dve.wait_ge(bias_done, part + 1)
                nc.vector.tensor_scalar(neg_bias[:, a:b], u_ps[:, a:b], b1, -1.0,
                                        ALU.add, ALU.mult).then_inc(setup_step, 1)

            def shifts():
                dve.wait_ge(shift_done, 1)
                each = Q // PARTS
                nc.vector.tensor_tensor(shift_sel[:, :, :],
                                        u_ps[:, 0:CHUNKS * each].rearrange("p (c r) -> p c r", r=each),
                                        own_row.unsqueeze(1).to_broadcast([P, CHUNKS, each]), ALU.mult).then_inc(u_free, 1)
                dve.wait_ge(u_free, 1)
                nc.vector.reduce_sum(shift[:, :], shift_sel[:, :, :], axis=AX.X).then_inc(setup_step, 1)
                dve.wait_ge(setup_step, 4)
                nc.vector.tensor_scalar(shift[:, :], shift[:, :], b2, None, ALU.add).then_inc(shift_made, 1)

            def low_half(c, q, k):
                w = GROUPS[k] * P
                h = xh[slot(q, k, "split")][:, 0:w]
                dve.wait_ge(xh_made, c * NG + (k + 1))
                nc.vector.tensor_tensor(xl[slot(q, k, "split")][:, 0:w], xt_ps[slot(q, k, "xt")][:, 0:w],
                                        h.bitcast(F32), ALU.subtract).then_inc(xl_made, 1)

            def biased_max(c, q, k, early):
                t = GROUPS[k]
                dve.wait_ge(z_done, c * NG + (k + 1))
                if k == 0 and not early:
                    dve.wait_ge(scores_done, c - 1)
                z = z_ps[slot(q, k, "z")][:, 0:t * P].rearrange("p (t b s) -> p t b s", b=ROWS, s=PARTS)
                nb = neg_bias[:, bass.ds(c * ROWS, ROWS)].unsqueeze(1).unsqueeze(3)
                nc.vector.tensor_tensor(hidden_view(q % 2, k), z, nb.to_broadcast([P, t, ROWS, PARTS]),
                                        ALU.max).then_inc(hidden_made, 1)

            def softmax(c, buf, step, early):
                done = c * SOFTMAX_STEPS + step
                if step == 0:
                    dve.wait_ge(scores_done, c + 1)
                    if not early:
                        dve.wait_ge(weights_made, c * 2 - 2)
                    op = nc.vector.transpose(scores[buf][:, :], s_ps[:, 0:RUN * Q])
                else:
                    dve.wait_ge(softmax_step, done)
                if step == 1:
                    if early:
                        dve.wait_ge(part_max_cleared, 1)
                    op = nc.vector.tensor_reduce(part_max[:, 0:1], score_runs(buf), axis=AX.XY, op=ALU.max)
                if step == 2:
                    op = nc.vector.transpose(part_max_t[:, :], part_max[:, :])
                if step == 3:
                    op = nc.vector.tensor_reduce(row_max_t[:, :], part_max_t[:, :].rearrange("p (b s) -> p b s", s=PARTS),
                                                 axis=AX.X, op=ALU.max)
                if step == 4:
                    op = nc.vector.tensor_copy(row_max_wide[:, :].rearrange("p (b s) -> p b s", s=PARTS),
                                               row_max_t[:, :].unsqueeze(2).to_broadcast([P, Q // PARTS, PARTS]))
                if step == 5:
                    op = nc.vector.transpose(row_max[:, :], row_max_wide[:, :])
                if step == 6:
                    own = shift[:, bass.ds(c, 1)]
                    op = nc.vector.scalar_tensor_tensor(exp_bias[buf][:, :], row_max[:, 0:1], own, own,
                                                        ALU.add, ALU.subtract, reverse1=True)
                op.then_inc(softmax_step, 1)

            def inverses(part, step):
                a, b = PART_CHUNKS[part]
                row_sums = inverse_ps[part]
                if step == 0:
                    dve.wait_ge(weights_made, 2 * b)
                    op = nc.vector.tensor_tensor(sums[:, a:b], weight_sums[:, a:b, 0], weight_sums[:, a:b, 1], ALU.add)
                if step == 1:
                    dve.wait_ge(row_sums_done, part + 1)
                    op = nc.vector.reciprocal(inv_sums[:, a:b], row_sums[:, 0:b - a])
                if step == 2:
                    dve.wait_ge(mlp_step, 4 * part + 2)
                    op = nc.vector.tensor_tensor(
                        inv_sel[:, a:b, :], inv_sums[:, a:b].unsqueeze(2).to_broadcast([P, b - a, ROWS]),
                        row_first.unsqueeze(1).to_broadcast([P, b - a, ROWS]), ALU.mult)
                op.then_inc(mlp_step, 1)

            def normalise(part):
                a, b = PART_CHUNKS[part]
                inv = inverse_ps[part]
                dve.wait_ge(inv_done, part + 1)
                dve.wait_ge(u_free, b + 1)
                nc.vector.tensor_tensor(pooled_n[:, a * ROWS:b * ROWS], inv[:, 0:(b - a) * ROWS],
                                        pooled_t[:, a * ROWS:b * ROWS], ALU.mult).then_inc(mlp_step, 1)

            low_half(0, 0, 0)
            low_half(0, 0, 1)
            negative_bias(0)
            dve.wait_ge(setup_step, 2)

            def period(c, q, phase):
                for k in range(NG):
                    if phase == 0 and k == BIAS_STEP:
                        negative_bias(1)
                    if k + LOW_AHEAD < NG:
                        low_half(c, q, k + LOW_AHEAD)
                    elif phase != CHUNKS - 1:
                        low_half(c + 1, (q + 1) % X_BUFS, k + LOW_AHEAD - NG)
                    if phase >= 1 and 1 <= k <= 4:
                        softmax(c - 1, (q + 1) % 2, 2 * (k - 1), phase <= 2)
                    biased_max(c, q, k, phase < 2)
                    if phase >= 1 and 1 <= k <= 3:
                        softmax(c - 1, (q + 1) % 2, 2 * (k - 1) + 1, phase <= 2)
                    if phase == 0 and k == SHIFT_STEP:
                        shifts()
                    if phase == CHUNKS - 1 and k == 4:
                        inverses(0, 0)

            periods(dve, period)
            last = CHUNKS - 1
            inverses(0, 1)
            inverses(0, 2)
            for step in range(SOFTMAX_STEPS):
                softmax(last, last % 2, step, False)
            normalise(0)

            def mask_last(run):
                a, b = [0, RUN, TILES][run:run + 2]
                buf = last % 2
                dve.wait_ge(weights_made, 2 * last + 1 + run)
                if run == 0:
                    dve.wait_ge(pooled_done, last)
                nc.vector.tensor_tensor(
                    weights_by_row[buf][:, a:b, pair_half[buf]],
                    weights[buf][:, a:b].unsqueeze(2).to_broadcast([P, b - a, ROWS]),
                    row_mask.unsqueeze(1).to_broadcast([P, b - a, ROWS]), ALU.mult).then_inc(last_masked, 1)

            mask_last(0)
            mask_last(1)
            for step in range(3):
                inverses(1, step)
            normalise(1)
            for part in range(2):
                dve.wait_ge(logit_done, part + 1)
                nc.vector.tensor_scalar(logit[:, part, 0:quarter[part]], logit_ps[:, 0:quarter[part]], b_out, None,
                                        ALU.add).then_inc(logit_made, 1)

        @block.tensor
        def _(pe):
            def transpose(c, q, k, loaded, early):
                if loaded is not None:
                    pe.wait_ge(loaded[0], loaded[1])
                if not early:
                    pe.wait_ge(xl_made, c * NG + (k + 1 - back(q, k, "xt")))
                for j in range(GROUPS[k]):
                    t = STARTS[k] + j
                    op = nc.tensor.transpose(xt_ps[slot(q, k, "xt")][:, j * P:(j + 1) * P],
                                             x[q][:, t * E:(t + 1) * E], ident)
                op.then_inc(transposed, 1)

            def products(c, q, k, early):
                w = GROUPS[k] * P
                s = slot(q, k, "split")
                z = z_ps[slot(q, k, "z")][:, 0:w]
                pe.wait_ge(xl_made, c * NG + (k + 1))
                if not early:
                    pe.wait_ge(hidden_made, c * NG + (k + 1 - back(q, k, "z")))
                nc.tensor.matmul(z, w_hi[:, :], xh[s][:, 0:w], start=True, stop=False)
                nc.tensor.matmul(z, w_lo[:, :], xh[s][:, 0:w], start=False, stop=False)
                nc.tensor.matmul(z, w_hi[:, :], xl[s][:, 0:w], start=False, stop=True).then_inc(z_done, 1)

            def score(c, buf, r, first):
                if first:
                    pe.wait_ge(f2_col_made, 2)
                pe.wait_ge(hidden_made, c * NG + (NG if r == 1 else FIRST_RUN_GROUPS))
                if r == 0 and not first:
                    pe.wait_ge(softmax_step, c * SOFTMAX_STEPS - (SOFTMAX_STEPS - 1))
                rows, t, n = [(Q, 0, RUN), (1, RUN, TILES - RUN)][r]
                for g in range(P // Q):
                    op = nc.tensor.matmul(
                        s_ps[g * Q:g * Q + rows, (RUN - n) * Q:RUN * Q].rearrange("p (t s) -> p t s", s=Q),
                        f2_col[:, 0:rows], hidden[buf][:, t:t + n, g * Q:(g + 1) * Q],
                        start=True, stop=True, tile_position=(0, g * Q))
                if r == 1:
                    op.then_inc(scores_done, 1)

            def sum_tile(bank, g, weights_ap, rows_ap, start, stop):
                return nc.tensor.matmul(bank[g * Q:(g + 1) * Q, 0:P], weights_ap, rows_ap,
                                        start=start, stop=stop, tile_position=(0, g * Q))

            def weighted_sum(c, q):
                buf = q % 2
                pe.wait_ge(pool_step, c * POOL_STEPS + POOL_STEPS)
                if buf == 0:
                    pe.wait_ge(u_free, c + 1)
                for g in range(SUMMED):
                    t = DIRECT + g
                    sum_tile(u_ps, g, weights_by_row[buf][:, t, :], x[q][:, t * E:(t + 1) * E], buf == 0, False)
                for g in range(SUMMED):
                    op = sum_tile(u_ps, g, pair_mask[buf], weighted[buf][:, g * E:(g + 1) * E], False, buf == 1)
                op.then_inc(pooled_done, 1)

            def weighted_sum_alone(c):
                buf = c % 2
                if buf == 0:
                    pe.wait_ge(pool_step, OFFLOADED * POOL_STEPS + 1)
                    pe.wait_ge(hidden_made, CHUNKS * NG)
                for t in range(TILES):
                    if buf == 1 and t in (0, RUN):
                        pe.wait_ge(last_masked, 1 + (t == RUN))
                    op = sum_tile(last_pair_ps, t % SUMMED, weights_by_row[buf][:, t, :],
                                  x[c % X_BUFS][:, t * E:(t + 1) * E], buf == 0 and t < SUMMED,
                                  buf == 1 and t >= TILES - SUMMED)
                op.then_inc(pooled_done, 1)

            def transpose_sums(c, bank):
                pe.wait_ge(pooled4_copied, c + 1)
                nc.tensor.matmul(bank[:, P:P + 2 * ROWS], pooled4[:, :], fold, start=True,
                                 stop=True).then_inc(pooled_t_done, 2)

            def shift_sums():
                pe.wait_ge(bias_f2_made, 1)
                each = Q // PARTS
                for g in range(P // Q):
                    op = nc.tensor.matmul(
                        u_ps[g * Q:(g + 1) * Q, 0:CHUNKS * each].rearrange("p (c r) -> p c r", r=each), ones[:, 0:Q],
                        bias_f2[:, :].rearrange("p (c r) -> p c r", r=ROWS)[:, :, g * each:(g + 1) * each],
                        start=True, stop=True, tile_position=(0, g * Q))
                op.then_inc(shift_done, 1)

            def row_sums(part):
                a, b = PART_CHUNKS[part]
                pe.wait_ge(mlp_step, 4 * part + 1)
                nc.tensor.matmul(inverse_ps[part][:, 0:b - a], same_row, sums[:, a:b],
                                 start=True, stop=True).then_inc(row_sums_done, 1)

            def spread_inverses(part):
                a, b = PART_CHUNKS[part]
                pe.wait_ge(mlp_step, 4 * part + 3)
                nc.tensor.matmul(inverse_ps[part][:, 0:(b - a) * ROWS], ones[:, :],
                                 inv_sel[:, a:b, :].rearrange("p c r -> p (c r)"),
                                 start=True, stop=True).then_inc(inv_done, 1)

            def mlp_candidates(part, m):
                a, b = (n * ROWS for n in PART_CHUNKS[part])
                if part == 0 and m == 0:
                    pe.wait_ge(later_loaded, 16)
                if part == 1 and m == 0:
                    pe.wait_ge(softmax_step, (CHUNKS - 1) * SOFTMAX_STEPS + 1)
                if part == 1 and m == 1:
                    pe.wait_ge(u_free, OFFLOADED + 1)
                nc.tensor.matmul(mlp_ps[part][m][:, 0:b - a], w_mlp[:, 1, m * P:(m + 1) * P], cand_t[:, a:b],
                                 start=True, stop=False)

            def mlp_pooled(part, m):
                a, b = (n * ROWS for n in PART_CHUNKS[part])
                pe.wait_ge(mlp_step, 4 * part + 4)
                nc.tensor.matmul(mlp_ps[part][m][:, 0:b - a], w_mlp[:, 0, m * P:(m + 1) * P], pooled_n[:, a:b],
                                 start=False, stop=True).then_inc(z_all_done, 1)

            def logits(part):
                if part == 1:
                    pe.wait_ge(logit_made, 1)
                for m in range(2):
                    pe.wait_ge(z_all_relu, 2 * part + m + 1)
                    for g in range(P // Q):
                        op = nc.tensor.matmul(logit_ps[g * Q:g * Q + 1, 0:quarter[part]], w_out[:, m:m + 1],
                                              z_all[:, m, bass.ds(PART_CHUNKS[part][0] * ROWS + g * quarter[part],
                                                                  quarter[part])],
                                              start=(m == 0), stop=(m == 1), tile_position=(0, g * Q))
                op.then_inc(logit_done, 1)

            def transpose_candidates(part):
                a, b = CAND_PARTS[part]
                pe.wait_ge(cand_loaded[part], 16)
                for n in range(a, b):
                    op = nc.tensor.transpose(s_ps[:, n * P:(n + 1) * P], cand[:, n, :], ident)
                op.then_inc(cand_t_done, 1)

            def bias_products(part):
                a, b = (n * P for n in CAND_PARTS[part])
                pe.wait_ge(cand_t_copied, part + 1)
                if part > 0:
                    pe.wait_ge(setup_step, 2)
                nc.tensor.matmul(u_ps[:, a:b], w_c, cand_t[:, a:b], start=True, stop=True).then_inc(bias_done, 1)

            pe.wait_ge(ones_made, 1)
            for n in range(WARM_UP):
                op = nc.tensor.matmul(z_ps[0][:, 0:P], ones[:, :], ones[:, :], start=True, stop=True)
            op.then_inc(pooled_done, 1)
            pe.wait_ge(first_loaded, 16)
            transpose(0, 0, 0, (x_piece[0], 16), True)
            transpose_candidates(0)
            transpose(0, 0, 1, (x_piece[1], 16), True)
            bias_products(0)
            transpose(0, 0, 2, (x_piece[2], 16), True)
            pe.wait_ge(w_lo_made, 1)

            def loads(c, q):
                return (c + (X_BUFS - q)) * (16 // X_BUFS)

            def period(c, q, phase):
                for k in range(NG):
                    products(c, q, k, phase == 0 and k < Z_BANKS)
                    if k + AHEAD < NG:
                        arrived = None
                        if phase == 0 and k == 0:
                            arrived = (x_loaded[0], 16)
                        if k + AHEAD == 5:
                            arrived = (x_rest_loaded[q], loads(c, q))
                        transpose(c, q, k + AHEAD, arrived, False)
                    elif phase != CHUNKS - 1:
                        nq = (q + 1) % X_BUFS
                        transpose(c + 1, nq, k + AHEAD - NG,
                                  (x_loaded[nq], loads(c + 1, nq)) if k == NG - AHEAD else None, False)
                    if k == 0 and phase >= 3:
                        weighted_sum(c - 3, (q + 1) % X_BUFS)
                    if k == 0 and phase >= 1:
                        score(c - 1, (q + 1) % 2, 1, False)
                    if k == 5:
                        score(c, q % 2, 0, phase == 0)
                    if k == 3 and phase >= 3 and (q - 3) % 2 == 1:
                        transpose_sums(c - 3, u_ps)
                    if k == 4 and phase == CHUNKS - 1:
                        mlp_candidates(0, 0)
                    if phase == 0 and k == 0:
                        transpose_candidates(1)
                    if phase == 0 and k == 1:
                        bias_products(1)
                    if phase == 0 and k == SUM_STEP:
                        shift_sums()
                    if phase == CHUNKS - 1 and k == 5:
                        row_sums(0)

            periods(pe, period)
            last = CHUNKS - 1
            mlp_candidates(0, 1)
            weighted_sum(last - 2, (last - 2) % X_BUFS)
            score(last, last % 2, 1, False)
            spread_inverses(0)
            transpose_sums(last - 2, u_ps)
            mlp_candidates(1, 0)
            weighted_sum_alone(last - 1)
            mlp_candidates(1, 1)
            weighted_sum_alone(last)
            row_sums(1)
            mlp_pooled(0, 0)
            transpose_sums(last, last_pair_ps)
            spread_inverses(1)
            mlp_pooled(0, 1)
            for m in range(2):
                mlp_pooled(1, m)
            logits(0)
            logits(1)


def layout_constants():
    import numpy as np

    p = np.arange(P)[:, None]
    rows = np.arange(P // PARTS)[None, :]
    row_mask = p // PARTS == rows
    zeros = np.zeros_like(row_mask)
    each = [p == p.T, np.concatenate([zeros, row_mask, zeros], axis=1), p % Q == np.arange(Q)[None, :],
            row_mask & (p % PARTS == 0), p % Q // PARTS == np.arange(Q // PARTS)[None, :],
            p // PARTS == p.T // PARTS]
    return [m.astype(np.float32) for m in each]


def kernel(r_behavior_emb, r_candidate_emb, L0_rec_fc1_w, L0_rec_fc1_b, L0_rec_fc2_w, L0_rec_fc2_b,
           L0_rec_mlp1_w, L0_rec_mlp1_b, L0_rec_mlp2_w, L0_rec_mlp2_b):
    import numpy as np
    import concourse.bacc as bacc
    from concourse.bass_utils import run_bass_kernel_spmd

    def column(v):
        v = np.asarray(v).reshape(-1)
        return np.broadcast_to(v, (P, 1)) if v.size == 1 else v.reshape(-1, P).T

    fc1_w, mlp1_w = np.asarray(L0_rec_fc1_w), np.asarray(L0_rec_mlp1_w)
    first = np.concatenate([*layout_constants(), fc1_w[:P], fc1_w[P:], column(L0_rec_fc1_b),
                            column(L0_rec_fc2_w), column(L0_rec_fc2_b)], axis=1)
    later = np.concatenate([mlp1_w[:P], mlp1_w[P:], column(L0_rec_mlp1_b), column(L0_rec_mlp2_w),
                            column(L0_rec_mlp2_b)], axis=1)
    arrays = {"behavior": r_behavior_emb, "candidate": r_candidate_emb, "first": first, "later": later}
    arrays = {f"in_{name}": np.ascontiguousarray(a) for name, a in arrays.items()}
    nc = bacc.Bacc("TRN2", target_bir_lowering=False, num_devices=1)
    args = [nc.dram_tensor(name, a.shape, mybir.dt.from_np(a.dtype), kind="ExternalInput").ap()
            for name, a in arrays.items()]
    args.append(nc.dram_tensor("out_logit", (r_behavior_emb.shape[0],), F32, kind="ExternalOutput").ap())
    attention_pooling_kernel(nc, *args)
    r = run_bass_kernel_spmd(nc, [arrays], core_ids=[0])
    return r.results[0]["out_logit"]
```
